# Optimizing a Trainium2 kernel written in Bass

```python
import numpy as np
import jax
import jax.numpy as jnp

def _softmax(x, axis=-1):
    return jax.nn.softmax(x, axis=axis)

def _gelu(x):
    return jax.nn.gelu(x, approximate=True)

def _silu(x):
    return jax.nn.silu(x)

def _sigmoid(x):
    return jax.nn.sigmoid(x)

def _layernorm(x, axis=-1, eps=1e-05):
    m = jnp.mean(x, axis=axis, keepdims=True)
    v = jnp.var(x, axis=axis, keepdims=True)
    return (x - m) / jnp.sqrt(v + eps)

def _scatter_add(tgt, idx, src, axis=0):
    return tgt.at[idx].add(src)

def _segment_sum(src, seg, n):
    return jax.ops.segment_sum(src, seg, n)
kernel_name = 'mk_adj_resnorm_d1_adj_r2_0a2b85'

def setup_inputs(seed: int=0):
    np.random.seed(seed)
    _w = jnp.asarray

    def _rec_inputs():
        import jax
        import jax.numpy as jnp
        _gk = jax.random.key(seed)
        x = -0.0001538 + 1 * jax.random.normal(jax.random.fold_in(_gk, 1), (64, 128, 384), jnp.float32)
        _a = jax.random.bernoulli(jax.random.fold_in(_gk, 2), 0.0625, (64, 128, 128))
        _a = jnp.logical_or(_a, jnp.swapaxes(_a, -1, -2))
        _a = jnp.logical_or(_a, jnp.eye(128, dtype=bool))
        _af = _a.astype(jnp.float32)
        _af = _af * jax.random.uniform(jax.random.fold_in(_gk, 3), (64, 128, 128), jnp.float32, 0.05, 5.06092)
        adj = _af
        return (x, adj)
    x, adj = _rec_inputs()

    def _L0_gnn_setup():
        import jax, jax.numpy as jnp
        import numpy as np
        D_MODEL = 384
        NHEADS = 8
        D_FF = 1536
        B, N = (8, 512)
        EPS = 1e-06

        def _rmsnorm(x, alpha, gamma):
            x = x * jax.lax.rsqrt(jnp.mean(x * x, axis=-1, keepdims=True) + EPS)
            return alpha * x + gamma
        key = jax.random.key(seed)
        ks = jax.random.split(key, 10)
        d, f = (D_MODEL, D_FF)
        s = 1.0 / np.sqrt(d)
        inp = {'x': jax.random.normal(ks[0], (B, N, d), dtype=jnp.float32), 'attn_bias': jax.random.normal(ks[1], (B, N, N), dtype=jnp.float32), 'wq': jax.random.normal(ks[2], (d, d), dtype=jnp.float32) * s, 'bq': jnp.zeros((d,), jnp.float32), 'wk': jax.random.normal(ks[3], (d, d), dtype=jnp.float32) * s, 'bk': jnp.zeros((d,), jnp.float32), 'wv': jax.random.normal(ks[4], (d, d), dtype=jnp.float32) * s, 'bv': jnp.zeros((d,), jnp.float32), 'wo': jax.random.normal(ks[5], (d, d), dtype=jnp.float32) * s, 'bo': jnp.zeros((d,), jnp.float32), 'w1': jax.random.normal(ks[6], (d, f), dtype=jnp.float32) * s, 'b1': jnp.zeros((f,), jnp.float32), 'w2': jax.random.normal(ks[7], (f, d), dtype=jnp.float32) * (1.0 / np.sqrt(f)), 'b2': jnp.zeros((d,), jnp.float32), 'alpha1': jnp.ones((d,), jnp.float32), 'gamma1': jnp.ones((d,), jnp.float32), 'alpha2': jnp.ones((d,), jnp.float32), 'gamma2': jnp.ones((d,), jnp.float32)}
        return inp
    _L0_gnn_all = _L0_gnn_setup()
    _L0_gnn_in = {k: v for k, v in _L0_gnn_all.items() if k in ('wq', 'bq', 'wk', 'bk', 'wv', 'bv', 'wo', 'bo', 'w1', 'b1', 'w2', 'b2', 'alpha1', 'gamma1', 'alpha2', 'gamma2')}
    del _L0_gnn_all
    return {'x': x, 'adj': adj, 'L0_gnn_wq': _L0_gnn_in['wq'], 'L0_gnn_bq': _L0_gnn_in['bq'], 'L0_gnn_wk': _L0_gnn_in['wk'], 'L0_gnn_bk': _L0_gnn_in['bk'], 'L0_gnn_wv': _L0_gnn_in['wv'], 'L0_gnn_bv': _L0_gnn_in['bv'], 'L0_gnn_wo': _L0_gnn_in['wo'], 'L0_gnn_bo': _L0_gnn_in['bo'], 'L0_gnn_w1': _L0_gnn_in['w1'], 'L0_gnn_b1': _L0_gnn_in['b1'], 'L0_gnn_w2': _L0_gnn_in['w2'], 'L0_gnn_b2': _L0_gnn_in['b2'], 'L0_gnn_alpha1': _L0_gnn_in['alpha1'], 'L0_gnn_gamma1': _L0_gnn_in['gamma1'], 'L0_gnn_alpha2': _L0_gnn_in['alpha2'], 'L0_gnn_gamma2': _L0_gnn_in['gamma2']}

def reference(x, adj, L0_gnn_wq, L0_gnn_bq, L0_gnn_wk, L0_gnn_bk, L0_gnn_wv, L0_gnn_bv, L0_gnn_wo, L0_gnn_bo, L0_gnn_w1, L0_gnn_b1, L0_gnn_w2, L0_gnn_b2, L0_gnn_alpha1, L0_gnn_gamma1, L0_gnn_alpha2, L0_gnn_gamma2):
    import jax
    import jax.numpy as jnp

    def _L0_gnn_ref(x, attn_bias, wq, bq, wk, bk, wv, bv, wo, bo, w1, b1, w2, b2, alpha1, gamma1, alpha2, gamma2):
        import jax, jax.numpy as jnp
        import numpy as np
        D_MODEL = 384
        NHEADS = 8
        D_FF = 1536
        B, N = (8, 512)
        EPS = 1e-06

        def _rmsnorm(x, alpha, gamma):
            x = x * jax.lax.rsqrt(jnp.mean(x * x, axis=-1, keepdims=True) + EPS)
            return alpha * x + gamma
        b, n, d = x.shape
        h = NHEADS
        dh = d // h
        scaling = dh ** (-0.5)

        def split_heads(t):
            return t.reshape(b, n, h, dh).transpose(0, 2, 1, 3)
        q = split_heads(x @ wq + bq)
        k = split_heads(x @ wk + bk)
        v = split_heads(x @ wv + bv)
        scores = jnp.einsum('bhqd,bhkd->bhqk', q, k) * scaling
        scores = scores + attn_bias[:, None, :, :]
        attn = jax.nn.softmax(scores, axis=-1)
        ctx = jnp.einsum('bhij,bhjd->bhid', attn, v)
        ctx = ctx.transpose(0, 2, 1, 3).reshape(b, n, d)
        attn_out = ctx @ wo + bo
        x = _rmsnorm(x + attn_out, alpha1, gamma1)
        ff = jax.nn.silu(x @ w1 + b1) @ w2 + b2
        x = _rmsnorm(x + ff, alpha2, gamma2)
        return x
    x = _layernorm(x + _L0_gnn_ref(x, adj, L0_gnn_wq, L0_gnn_bq, L0_gnn_wk, L0_gnn_bk, L0_gnn_wv, L0_gnn_bv, L0_gnn_wo, L0_gnn_bo, L0_gnn_w1, L0_gnn_b1, L0_gnn_w2, L0_gnn_b2, L0_gnn_alpha1, L0_gnn_gamma1, L0_gnn_alpha2, L0_gnn_gamma2), axis=-1)
    return x

_drawn_inputs = setup_inputs


def setup_inputs(seed=0):
    import zlib

    import numpy as np

    out = dict(_drawn_inputs(seed))
    spreads = {'L0_gnn_bq': (0.0, 0.676),
     'L0_gnn_bk': (0.0, 0.8),
     'L0_gnn_bv': (0.0, 0.1),
     'L0_gnn_bo': (0.0, 0.1),
     'L0_gnn_b1': (0.0, 0.338),
     'L0_gnn_b2': (0.0, 0.1),
     'L0_gnn_alpha1': (1.0, 0.2),
     'L0_gnn_gamma1': (1.0, 0.2),
     'L0_gnn_alpha2': (1.0, 0.2),
     'L0_gnn_gamma2': (1.0, 0.2)}
    factors = {}
    for name, (base, spread) in spreads.items():
        noise = np.random.default_rng([zlib.crc32(name.encode()), seed]).standard_normal(out[name].shape)
        drawn = base * np.exp(spread * noise) if base else spread * noise
        out[name] = jnp.asarray(drawn.astype(out[name].dtype))
    for name, factor in factors.items():
        out[name] = (out[name] * factor).astype(out[name].dtype)
    return out
```

```python
from contextlib import ExitStack

import concourse.bass as bass
from concourse import mybir

P = 128
F32 = mybir.dt.float32
F32R = mybir.dt.float32r
ALU = mybir.AluOpType
ACT = mybir.ActivationFunctionType
AX_X = mybir.AxisListType.X

HEADS = 8
TILES = 2
RMS_EPS = 1e-6
LN_EPS = 1e-5

COL_NAMES = ("bq", "bk", "b1", "alpha1", "gamma1")
ROW_NAMES = ("bv", "bo", "alpha1", "gamma1", "b2", "alpha2", "gamma2")

SCORES_AT = (1, 8)
EXP_AT = (3, 10)
PT_AT = (6, 13)
CTX_AT = (8, 15)
CTXT_AT = (9, 16)
WO_AT = (11, 18)
YN_AT = (12, 19)
X1T_AT = (14, 21)
X1SPLIT_AT = (15, 22)
XT_SPLIT_AT = 17


class Signal:

    def __init__(self, sem, n, primed=False):
        self.sem, self.n, self.primed = sem, n, primed

    def at(self, group, event):
        i, offset = group
        return i * self.n + (offset + self.primed) * self.n + event


def build(nc, xT_d, x_d, adj_d, watt_d, w1_d, w2_d, cols_d, rows_d, ident_d, out_d):
    G = x_d.shape[0]
    D = watt_d.shape[0]
    FF = w1_d.shape[1]
    KD = D // P
    KF = FF // P
    DH = D // HEADS
    NT = TILES * P
    SCALE = float(DH) ** -0.5
    UNIT = 4 * D
    assert UNIT == FF and KF % 4 == 0
    UNITS = 2 * KD + KF // 4
    QK = 2 * KD
    F2_PARTS = KF // 2
    SLOTS = KF + TILES * F2_PARTS
    HALF = HEADS // 2
    PAIRS = KD

    col_at, at = {}, 0
    for name in COL_NAMES:
        col_at[name] = at
        at += KF if name == "b1" else KD

    with ExitStack() as ctx:

        def sb(name, shape, dt=F32):
            return ctx.enter_context(nc.sbuf_tensor(name, shape, dt))

        def ps(name, shape):
            return ctx.enter_context(nc.psum_tensor(name, shape, F32))

        def signal(name, n, primed=False):
            return Signal(ctx.enter_context(nc.semaphore(name)), n, primed)

        w_hi = sb("w_hi", [P, UNITS, UNIT], F32R)
        w_lo = sb("w_lo", [P, UNITS, UNIT], F32R)
        cols = sb("cols", [P, at])
        cols_scaled = sb("cols_scaled", [P, KD + KF])
        rows = sb("rows", [P, len(ROW_NAMES), D])
        ident = sb("ident", [P, P])
        minus_half = sb("minus_half", [P, 1])
        rms_eps = sb("rms_eps", [P, 1])
        ln_eps = sb("ln_eps", [P, 1])

        xT = sb("xT", [P, KD, NT])
        xT_hi = sb("xT_hi", [P, KD, NT], F32R)
        xT_lo = sb("xT_lo", [P, KD, NT], F32R)
        x = sb("x", [P, TILES, D])
        x_gamma2 = sb("x_gamma2", [P, TILES, D])
        adj = sb("adj", [P, TILES, P])
        qkT = sb("qkT", [P, QK, NT])
        qkT_last = sb("qkT_last", [P, 2, NT])
        v = sb("v", [P, TILES, HEADS, DH + 1])
        probs = sb("probs", [P, HEADS, P])
        probsT = sb("probsT", [P, HEADS, P])
        neg_max = sb("neg_max", [P, HEADS])
        inv_sum = sb("inv_sum", [P, HEADS])
        context = sb("context", [P, D])
        ctxT_hi = sb("ctxT_hi", [P, KD, P], F32R)
        ctxT_lo = sb("ctxT_lo", [P, KD, P], F32R)
        y1 = sb("y1", [P, TILES, D])
        x1T = sb("x1T", [P, KD, P])
        x1T_hi = sb("x1T_hi", [P, KD, NT], F32R)
        x1T_lo = sb("x1T_lo", [P, KD, NT], F32R)
        hT_hi = sb("hT_hi", [P, KF, NT], F32R)
        hT_lo = sb("hT_lo", [P, KF, NT], F32R)
        squares = sb("squares", [P, D])
        stats = sb("stats", [P, 2, 3])
        bn = sb("bn", [P, 6])
        moments = sb("moments", [P, 2])
        ln_stats = sb("ln_stats", [P, 2])
        ffn_scratch = sb("ffn_scratch", [P, UNIT])
        tail_scratch = sb("tail_scratch", [P, UNIT])
        stage = (ffn_scratch, tail_scratch)
        half_z = ffn_scratch[:, 0 : 2 * NT].rearrange("p (r n) -> p r n", r=2)
        tanh_z = ffn_scratch[:, 2 * NT : 4 * NT].rearrange("p (r n) -> p r n", r=2)
        hT = ffn_scratch[:, 4 * NT : 6 * NT].rearrange("p (r n) -> p r n", r=2)
        x1_b2 = tail_scratch[:, 0 : TILES * D].rearrange("p (t n) -> p t n", t=TILES)
        y2 = tail_scratch[:, TILES * D : 2 * TILES * D].rearrange("p (t n) -> p t n", t=TILES)

        main = ps("main", [P, 2, 512])
        scores = ps("scores", [P, HEADS * P])
        probsT_ps = ps("probsT_ps", [P, HEADS * P])
        small = ps("small", [P, 2, 512])

        weights_in = [signal(f"weights_in{n}", 0) for n in range(2)]
        consts_in = signal("consts_in", 0)
        xT_in = signal("xT_in", 16)
        x_in = signal("x_in", 16)
        adj_in = signal("adj_in", 16)
        heads_moved = signal("heads_moved", 16 * 2 * PAIRS)
        out_stored = [signal(f"out_stored{t}", 16, primed=True) for t in range(TILES)]
        w_hi_done = signal("w_hi_done", 0)
        w_lo_done = signal("w_lo_done", 0)
        consts_ready = signal("consts_ready", 0)
        qk_done = signal("qk_done", QK)
        v_done = signal("v_done", TILES)
        scores_done = signal("scores_done", TILES)
        pt_done = signal("pt_done", TILES)
        ctx_done = signal("ctx_done", TILES)
        ctxT_done = signal("ctxT_done", TILES)
        wo_done = signal("wo_done", TILES)
        x1T_done = signal("x1T_done", TILES)
        f1_done = signal("f1_done", KF)
        f2_done = signal("f2_done", TILES)
        qk_evacuated = signal("qk_evacuated", QK)
        exp_done = signal("exp_done", TILES)
        pt_evacuated = signal("pt_evacuated", TILES)
        ctxT_hi_done = signal("ctxT_hi_done", TILES)
        squares1_done = signal("squares1_done", TILES)
        y1_normalized = signal("y1_normalized", TILES)
        x1T_evacuated = signal("x1T_evacuated", TILES, primed=True)
        half_z_done = signal("half_z_done", KF)
        tanh_done = signal("tanh_done", KF)
        squares2_done = signal("squares2_done", TILES)
        xT_hi_done = signal("xT_hi_done", 1)
        xT_split = signal("xT_split", 1)
        v_evacuated = signal("v_evacuated", TILES)
        scores_biased = signal("scores_biased", TILES, primed=True)
        max_done = signal("max_done", TILES)
        inv_sum_done = signal("inv_sum_done", TILES)
        context_done = signal("context_done", TILES)
        ctxT_lo_done = signal("ctxT_lo_done", TILES)
        y1_done = signal("y1_done", TILES, primed=True)
        x1T_hi_done = signal("x1T_hi_done", TILES)
        x1T_split = signal("x1T_split", TILES, primed=True)
        hT_done = signal("hT_done", KF, primed=True)
        hT_hi_done = signal("hT_hi_done", KF)
        hT_split = signal("hT_split", KF, primed=True)
        y2_done = signal("y2_done", TILES, primed=True)
        x2_done = signal("x2_done", TILES)
        z_done = signal("z_done", TILES, primed=True)
        bn_done = signal("bn_done", TILES)
        moments_done = signal("moments_done", TILES)
        out_ready = signal("out_ready", TILES)
        x_gamma2_done = signal("x_gamma2_done", 1)
        x_bo_done = signal("x_bo_done", 1)
        x1_scaled = signal("x1_scaled", TILES, primed=True)
        x1_b2_done = signal("x1_b2_done", TILES)
        mean1_done = signal("mean1_done", TILES)
        rstd1_done = signal("rstd1_done", TILES)
        mean2_done = signal("mean2_done", TILES)
        rstd2_done = signal("rstd2_done", TILES)
        var_done = signal("var_done", TILES)
        rstd3_done = signal("rstd3_done", TILES)

        def row(name):
            return rows[:, ROW_NAMES.index(name), :]

        def col(name, c):
            return cols[:, col_at[name] + c : col_at[name] + c + 1]

        def plain(ap):
            return ap.bitcast(F32)

        def tokens(t):
            return slice(t * P, (t + 1) * P)

        def dram_group(ap, group):
            i, offset = group
            return ap[bass.ds(i + offset, 1), :, :].rearrange("g p n -> (g p) n")

        def weight_source(unit):
            if unit < KD:
                return watt_d[unit * P : (unit + 1) * P, :]
            if unit < 2 * KD:
                return w1_d[(unit - KD) * P : (unit - KD + 1) * P, :]
            first = (unit - 2 * KD) * 4 * P
            return w2_d[first : first + 4 * P, :].rearrange("(f p) n -> p f n", p=P)

        def w2_cols(f):
            return 2 * KD + f // 4, slice((f % 4) * D, (f % 4 + 1) * D)

        def all_iterations(engine, iteration):
            iteration(-1, True, False, True)
            with engine.Fori(0, G - 2) as i:
                iteration(i, True, True, True)
            iteration(G - 2, True, True, False)
            iteration(G - 1, False, True, False)

        block = ctx.enter_context(nc.Block())

        @block.sync
        def _(sp):
            for t in range(TILES):
                sp.sem_inc(out_stored[t].sem, 16)
            sp.dma_start(xT[:, :, :], dram_group(xT_d, (0, 0)).rearrange("p (k n) -> p k n", k=KD)).then_inc(xT_in.sem, 16)
            for unit in range(UNITS):
                if unit >= 2:
                    sp.wait_ge(w_hi_done.sem, unit - 1)
                    sp.wait_ge(w_lo_done.sem, unit - 1)
                dst = stage[unit % 2][:, :]
                if unit >= 2 * KD:
                    dst = dst.rearrange("p (f n) -> p f n", f=4)
                sp.dma_start(dst, weight_source(unit)).then_inc(weights_in[unit % 2].sem, 16)
                if unit == 1:
                    sp.dma_start(cols[:, :], cols_d).then_inc(consts_in.sem, 16)
                    sp.dma_start(rows[:, :, :], rows_d).then_inc(consts_in.sem, 16)
                    sp.dma_start(ident[:, :], ident_d).then_inc(consts_in.sem, 16)

            def iteration(i, attention, ffn, following):
                this, att, nxt = (i, 0), (i, 1), (i, 2)
                if following:
                    sp.wait_ge(xT_split.sem, xT_split.at(att, 1))
                    sp.dma_start(xT[:, :, :], dram_group(xT_d, nxt).rearrange("p (k n) -> p k n", k=KD)).then_inc(xT_in.sem, 16)
                if attention:
                    if ffn:
                        sp.wait_ge(x_gamma2_done.sem, x_gamma2_done.at(this, 1))
                        sp.wait_ge(scores_biased.sem, scores_biased.at(this, TILES))
                    sp.dma_start(x[:, :, :], dram_group(x_d, att).rearrange("p (t n) -> p t n", t=TILES)).then_inc(x_in.sem, 16)
                    sp.dma_start(adj[:, :, :], dram_group(adj_d, att).rearrange("p (t n) -> p t n", t=TILES)).then_inc(adj_in.sem, 16)
                    sp.wait_ge(qk_evacuated.sem, qk_evacuated.at(att, QK))
                    spare = DH // PAIRS
                    for c in range(PAIRS):
                        for half in (0, 64):
                            sp.dma_start(
                                qkT_last[half + c * spare : half + (c + 1) * spare, :, :],
                                qkT[half + DH : half + DH + spare, c::KD, :],
                            ).then_inc(heads_moved.sem, 16)
                if ffn:
                    for t in range(TILES):
                        sp.wait_ge(out_ready.sem, out_ready.at(this, t + 1))
                        sp.dma_start(
                            dram_group(out_d, this)[:, t * D : (t + 1) * D], y2[:, t, :]
                        ).then_inc(out_stored[t].sem, 16)

            all_iterations(sp, iteration)
            for t in range(TILES):
                sp.wait_ge(out_stored[t].sem, out_stored[t].at((G - 1, 0), 16))

        @block.tensor
        def _(pe):
            HI_LO = ((0, 0), (0, 1), (1, 0))

            def product(out, left, right, steps, first, last):
                for n, step in enumerate(steps):
                    for m, (a, b) in enumerate(HI_LO):
                        done = nc.tensor.matmul(
                            out,
                            left[a](step),
                            right[b](step),
                            start=first and n == 0 and m == 0,
                            stop=last and n == len(steps) - 1 and m == 2,
                        )
                return done

            def qkv(i, ffn):
                before, this, att = (i, -1), (i, 0), (i, 1)
                pe.wait_ge(xT_split.sem, xT_split.at(att, 1))
                for n in range(QK):
                    if n < 2 and ffn:
                        pe.wait_ge(y2_done.sem, y2_done.at(before, n + 1))
                        pe.wait_ge(v_evacuated.sem, v_evacuated.at(this, n + 1))
                    if n >= 2:
                        pe.wait_ge(qk_evacuated.sem, qk_evacuated.at(att, n - 1))
                    product(
                        main[:, n % 2, 0:NT],
                        [lambda k, w=w: w[:, k, tokens(n)] for w in (w_hi, w_lo)],
                        [lambda k, a=a: a[:, k, :] for a in (xT_hi, xT_lo)],
                        range(KD), True, True,
                    ).then_inc(qk_done.sem, 1)
                for t in range(TILES):
                    pe.wait_ge(qk_evacuated.sem, qk_evacuated.at(att, QK - 1 + t))
                    product(
                        main[:, t, 0:D],
                        [lambda k, a=a: a[:, k, tokens(t)] for a in (xT_hi, xT_lo)],
                        [lambda k, w=w: w[:, k, 2 * D : 3 * D] for w in (w_hi, w_lo)],
                        range(KD), True, True,
                    ).then_inc(v_done.sem, 1)

            def score_step(att, t):
                if t == 0:
                    pe.wait_ge(qk_evacuated.sem, qk_evacuated.at(att, QK))
                    pe.wait_ge(heads_moved.sem, heads_moved.at(att, heads_moved.n))
                if t == 0:
                    pe.wait_ge(scores_biased.sem, scores_biased.at((att[0], att[1] - 1), TILES))
                else:
                    pe.wait_ge(scores_biased.sem, scores_biased.at(att, t))
                for h in range(HEADS):
                    c, odd = divmod(h, 2)
                    at = slice(64 * odd, 64 * odd + DH)
                    if c < PAIRS:
                        q, k = qkT[at, c, tokens(t)], qkT[at, KD + c, tokens(t)]
                    else:
                        q, k = qkT_last[at, 0, tokens(t)], qkT_last[at, 1, tokens(t)]
                    j = odd * HALF + c
                    done = nc.tensor.matmul(scores[:, tokens(j)], q, k, start=True, stop=True)
                done.then_inc(scores_done.sem, 1)

            def transpose_probs(att, t):
                pe.wait_ge(exp_done.sem, exp_done.at(att, t + 1))
                for j in range(HEADS):
                    done = nc.tensor.transpose(probsT_ps[:, tokens(j)], probs[:, j, :], ident[:, :])
                done.then_inc(pt_done.sem, 1)

            def context_step(att, t):
                pe.wait_ge(pt_evacuated.sem, pt_evacuated.at(att, t + 1))
                if t == 0:
                    pe.wait_ge(v_evacuated.sem, v_evacuated.at(att, TILES))
                    pe.wait_ge(y1_done.sem, y1_done.at((att[0], att[1] - 1), TILES))
                else:
                    pe.wait_ge(y1_done.sem, y1_done.at(att, t))
                for h in range(HEADS):
                    j = (h % 2) * HALF + h // 2
                    done = nc.tensor.matmul(
                        small[:, 0, h * (DH + 1) : (h + 1) * (DH + 1)],
                        probsT[:, j, :], v[:, t, h, :], start=True, stop=True,
                    )
                done.then_inc(ctx_done.sem, 1)

            def transpose_context(att, t):
                pe.wait_ge(context_done.sem, context_done.at(att, t + 1))
                if t == 0:
                    pe.wait_ge(x1T_evacuated.sem, x1T_evacuated.at((att[0], att[1] - 1), TILES))
                else:
                    pe.wait_ge(x1T_evacuated.sem, x1T_evacuated.at(att, t))
                for c in range(KD):
                    done = nc.tensor.transpose(small[:, 1, tokens(c)], context[:, tokens(c)], ident[:, :])
                done.then_inc(ctxT_done.sem, 1)

            def output_projection(att, t):
                pe.wait_ge(ctxT_lo_done.sem, ctxT_lo_done.at(att, t + 1))
                product(
                    small[:, 0, 0:D],
                    [lambda k, a=a: a[:, k, :] for a in (ctxT_hi, ctxT_lo)],
                    [lambda k, w=w: w[:, k, 3 * D : 4 * D] for w in (w_hi, w_lo)],
                    range(KD), True, True,
                ).then_inc(wo_done.sem, 1)

            def transpose_x1(att, t):
                pe.wait_ge(y1_normalized.sem, y1_normalized.at(att, t + 1))
                for c in range(KD):
                    done = nc.tensor.transpose(small[:, 1, tokens(c)], y1[:, t, tokens(c)], ident[:, :])
                done.then_inc(x1T_done.sem, 1)

            def ffn_up(this, f):
                if f == 0:
                    pe.wait_ge(x1T_split.sem, x1T_split.at(this, TILES))
                if f >= 2:
                    pe.wait_ge(half_z_done.sem, half_z_done.at(this, f - 1))
                product(
                    main[:, f % 2, 0:NT],
                    [lambda k, w=w: w[:, KD + k, tokens(f)] for w in (w_hi, w_lo)],
                    [lambda k, a=a: a[:, k, :] for a in (x1T_hi, x1T_lo)],
                    range(KD), True, True,
                ).then_inc(f1_done.sem, 1)

            def ffn_down(this, t, part):
                if part == 0:
                    pe.wait_ge(half_z_done.sem, half_z_done.at(this, KF - 1 + t))
                for f in (2 * part, 2 * part + 1):
                    if t == 0:
                        pe.wait_ge(hT_split.sem, hT_split.at(this, f + 1))
                last = part == F2_PARTS - 1
                done = product(
                    main[:, t, 0:D],
                    [lambda f, a=a: a[:, f, tokens(t)] for a in (hT_hi, hT_lo)],
                    [lambda f, w=w: w[:, w2_cols(f)[0], w2_cols(f)[1]] for w in (w_hi, w_lo)],
                    (2 * part, 2 * part + 1), part == 0, last,
                )
                if last:
                    done.then_inc(f2_done.sem, 1)

            def iteration(i, attention, ffn, following):
                this, att = (i, 0), (i, 1)
                if attention:
                    qkv(i, ffn)
                if ffn and attention:
                    pe.wait_ge(v_evacuated.sem, v_evacuated.at(att, TILES))
                elif ffn:
                    pe.wait_ge(y2_done.sem, y2_done.at((i, -1), TILES))
                for slot in range(SLOTS):
                    for t in range(TILES):
                        if attention and slot == SCORES_AT[t]:
                            score_step(att, t)
                        if attention and slot == PT_AT[t]:
                            transpose_probs(att, t)
                        if attention and slot == CTX_AT[t]:
                            context_step(att, t)
                        if attention and slot == CTXT_AT[t]:
                            transpose_context(att, t)
                        if attention and slot == WO_AT[t]:
                            output_projection(att, t)
                        if attention and slot == X1T_AT[t]:
                            transpose_x1(att, t)
                    if ffn and slot < KF:
                        ffn_up(this, slot)
                    if ffn and slot >= KF:
                        ffn_down(this, *divmod(slot - KF, F2_PARTS))

            pe.wait_ge(w_hi_done.sem, KD)
            pe.wait_ge(w_lo_done.sem, KD)
            pe.wait_ge(consts_ready.sem, 1)
            iteration(-1, True, False, True)
            pe.wait_ge(w_hi_done.sem, UNITS)
            pe.wait_ge(w_lo_done.sem, UNITS)
            with pe.Fori(0, G - 2) as i:
                iteration(i, True, True, True)
            iteration(G - 2, True, True, False)
            iteration(G - 1, False, True, False)

        @block.scalar
        def _(act):
            act.sem_inc(x1T_evacuated.sem, TILES)

            def split_hi(unit):
                act.wait_ge(weights_in[unit % 2].sem, 16 * (unit // 2 + 1))
                nc.scalar.copy(w_hi[:, unit, :], stage[unit % 2][:, :]).then_inc(w_hi_done.sem, 1)

            def evacuate_qk(att, n):
                act.wait_ge(qk_done.sem, qk_done.at(att, n + 1))
                c = n % KD
                if n < KD:
                    bias, scale = cols_scaled[:, c : c + 1], SCALE
                else:
                    bias, scale = col("bk", c), 1.0
                nc.scalar.activation(qkT[:, n, :], main[:, n % 2, 0:NT], ACT.Identity, bias=bias, scale=scale).then_inc(qk_evacuated.sem, 1)

            def exponentials(att, t):
                act.wait_ge(max_done.sem, max_done.at(att, t + 1))
                for j in range(HEADS):
                    done = nc.scalar.activation(probs[:, j, :], probs[:, j, :], ACT.Exp, bias=neg_max[:, j : j + 1])
                done.then_inc(exp_done.sem, 1)

            def evacuate_probsT(att, t):
                act.wait_ge(pt_done.sem, pt_done.at(att, t + 1))
                nc.scalar.copy(probsT[:, :, :], probsT_ps[:, :].rearrange("p (j n) -> p j n", j=HEADS)).then_inc(pt_evacuated.sem, 1)

            def context_hi(att, t):
                act.wait_ge(ctxT_done.sem, ctxT_done.at(att, t + 1))
                nc.scalar.copy(ctxT_hi[:, :, :], small[:, 1, 0:D].rearrange("p (c n) -> p c n", c=KD)).then_inc(ctxT_hi_done.sem, 1)

            def squares1(att, t):
                act.wait_ge(y1_done.sem, y1_done.at(att, t + 1))
                nc.scalar.activation(squares[:, :], y1[:, t, :], ACT.Square, scale=D**-0.5, accum_out=stats[:, 0, 0:1]).then_inc(squares1_done.sem, 1)

            def normalize1(att, t):
                act.wait_ge(rstd1_done.sem, rstd1_done.at(att, t + 1))
                nc.scalar.activation(y1[:, t, :], y1[:, t, :], ACT.Copy, scale=stats[:, 0, 2:3]).then_inc(y1_normalized.sem, 1)

            def evacuate_x1T(att, t):
                act.wait_ge(x1T_done.sem, x1T_done.at(att, t + 1))
                if t == 0:
                    act.wait_ge(x1T_split.sem, x1T_split.at((att[0], att[1] - 1), TILES))
                else:
                    act.wait_ge(x1T_split.sem, x1T_split.at(att, t))
                for c in range(KD):
                    done = nc.scalar.activation(x1T[:, c, :], small[:, 1, tokens(c)], ACT.Identity, bias=col("gamma1", c), scale=col("alpha1", c))
                done.then_inc(x1T_evacuated.sem, 1)

            def silu_parts(this, f):
                act.wait_ge(f1_done.sem, f1_done.at(this, f + 1))
                if f >= 2:
                    act.wait_ge(hT_done.sem, hT_done.at(this, f - 1))
                else:
                    act.wait_ge(hT_done.sem, hT_done.at((this[0], this[1] - 1), KF - 1 + f))
                nc.scalar.activation(half_z[:, f % 2, :], main[:, f % 2, 0:NT], ACT.Identity, bias=cols_scaled[:, KD + f : KD + f + 1], scale=0.5).then_inc(half_z_done.sem, 1)
                act.wait_ge(half_z_done.sem, half_z_done.at(this, f + 1))
                nc.scalar.activation(tanh_z[:, f % 2, :], half_z[:, f % 2, :], ACT.Tanh).then_inc(tanh_done.sem, 1)

            def squares2(this, t):
                act.wait_ge(y2_done.sem, y2_done.at(this, t + 1))
                nc.scalar.activation(squares[:, :], y2[:, t, :], ACT.Square, scale=D**-0.5, accum_out=stats[:, 1, 0:1]).then_inc(squares2_done.sem, 1)

            def iteration(i, attention, ffn, following):
                this, att = (i, 0), (i, 1)
                if attention:
                    for n in range(QK):
                        evacuate_qk(att, n)
                for slot in range(SLOTS):
                    for t in range(TILES):
                        if attention and slot == EXP_AT[t]:
                            exponentials(att, t)
                        if attention and slot == PT_AT[t]:
                            evacuate_probsT(att, t)
                        if attention and slot == CTXT_AT[t]:
                            context_hi(att, t)
                        if attention and slot == WO_AT[t]:
                            if ffn and slot >= KF + F2_PARTS:
                                act.wait_ge(squares2_done.sem, squares2_done.at(this, 1))
                            squares1(att, t)
                        if attention and slot == YN_AT[t]:
                            normalize1(att, t)
                        if attention and slot == X1T_AT[t]:
                            evacuate_x1T(att, t)
                    if ffn and slot < KF:
                        silu_parts(this, slot)
                    if ffn and slot >= KF and (slot - KF + 1) % F2_PARTS == 0:
                        squares2(this, (slot - KF) // F2_PARTS)

            for unit in range(UNITS):
                split_hi(unit)
            act.wait_ge(consts_ready.sem, 1)
            all_iterations(act, iteration)

        @block.vector
        def _(dve):
            for s in (scores_biased, y1_done, x1T_split, hT_done, hT_split, y2_done, z_done):
                dve.sem_inc(s.sem, s.n)

            def split(source, hi, lo, hi_done, lo_done, group, event):
                nc.vector.tensor_copy(hi, source).then_inc(hi_done.sem, 1)
                dve.wait_ge(hi_done.sem, hi_done.at(group, event))
                nc.vector.tensor_tensor(lo, source, plain(hi), ALU.subtract).then_inc(lo_done.sem, 1)

            def split_xT(group):
                dve.wait_ge(xT_in.sem, xT_in.at(group, 16))
                split(xT[:, :, :], xT_hi[:, :, :], xT_lo[:, :, :], xT_hi_done, xT_split, group, 1)

            def prepare_constants():
                dve.wait_ge(consts_in.sem, 48)
                nc.vector.tensor_scalar(cols_scaled[:, 0:KD], cols[:, 0:KD], SCALE, None, ALU.mult)
                nc.vector.tensor_scalar(cols_scaled[:, KD:], cols[:, col_at["b1"] : col_at["b1"] + KF], 0.5, None, ALU.mult)
                nc.vector.memset(v[:, :, :, DH : DH + 1], 1.0)
                nc.vector.memset(minus_half[:, :], -0.5)
                nc.vector.memset(rms_eps[:, :], RMS_EPS)
                nc.vector.memset(ln_eps[:, :], LN_EPS)
                nc.vector.tensor_tensor(row("b2"), row("b2"), row("gamma1"), ALU.add).then_inc(consts_ready.sem, 1)

            def evacuate_v(att, t):
                dve.wait_ge(v_done.sem, v_done.at(att, t + 1))
                nc.vector.tensor_tensor(
                    v[:, t, :, 0:DH],
                    main[:, t, 0:D].rearrange("p (h d) -> p h d", h=HEADS),
                    row("bv").rearrange("p (h d) -> p h d", h=HEADS), ALU.add,
                ).then_inc(v_evacuated.sem, 1)

            def bias_and_max(att, t):
                dve.wait_ge(scores_done.sem, scores_done.at(att, t + 1))
                if t == 0:
                    dve.wait_ge(adj_in.sem, adj_in.at(att, 16))
                nc.vector.tensor_tensor(
                    probs[:, :, :],
                    scores[:, :].rearrange("p (j n) -> p j n", j=HEADS),
                    adj[:, t : t + 1, :].to_broadcast([P, HEADS, P]), ALU.add,
                ).then_inc(scores_biased.sem, 1)
                dve.wait_ge(scores_biased.sem, scores_biased.at(att, t + 1))
                nc.vector.tensor_reduce(neg_max[:, :], probs[:, :, :], AX_X, ALU.max, negate=True).then_inc(max_done.sem, 1)

            def normalize_context(att, t):
                dve.wait_ge(ctx_done.sem, ctx_done.at(att, t + 1))
                sums = small[:, 0, 0 : HEADS * (DH + 1)].rearrange("p (h d) -> p h d", h=HEADS)
                nc.vector.reciprocal(inv_sum[:, :], sums[:, :, DH : DH + 1].rearrange("p h o -> p (h o)")).then_inc(inv_sum_done.sem, 1)
                dve.wait_ge(inv_sum_done.sem, inv_sum_done.at(att, t + 1))
                nc.vector.tensor_tensor(
                    context[:, :].rearrange("p (h d) -> p h d", h=HEADS),
                    sums[:, :, 0:DH],
                    inv_sum[:, :].unsqueeze(2).to_broadcast([P, HEADS, DH]), ALU.mult,
                ).then_inc(context_done.sem, 1)

            def context_lo(att, t):
                dve.wait_ge(ctxT_hi_done.sem, ctxT_hi_done.at(att, t + 1))
                nc.vector.tensor_tensor(
                    ctxT_lo[:, :, :], small[:, 1, 0:D].rearrange("p (c n) -> p c n", c=KD),
                    plain(ctxT_hi[:, :, :]), ALU.subtract,
                ).then_inc(ctxT_lo_done.sem, 1)

            def residual1(att, t):
                dve.wait_ge(wo_done.sem, wo_done.at(att, t + 1))
                if t == 0:
                    dve.wait_ge(x_bo_done.sem, x_bo_done.at(att, 1))
                nc.vector.tensor_tensor(y1[:, t, :], small[:, 0, 0:D], y1[:, t, :], ALU.add).then_inc(y1_done.sem, 1)

            def split_x1T(att, t):
                dve.wait_ge(x1T_evacuated.sem, x1T_evacuated.at(att, t + 1))
                split(x1T[:, :, :], x1T_hi[:, :, tokens(t)], x1T_lo[:, :, tokens(t)], x1T_hi_done, x1T_split, att, t + 1)

            def silu(this, f):
                dve.wait_ge(tanh_done.sem, tanh_done.at(this, f + 1))
                if f >= 2:
                    dve.wait_ge(hT_split.sem, hT_split.at(this, f - 1))
                else:
                    dve.wait_ge(hT_split.sem, hT_split.at((this[0], this[1] - 1), KF - 1 + f))
                nc.vector.scalar_tensor_tensor(
                    hT[:, f % 2, :], tanh_z[:, f % 2, :], 1.0, half_z[:, f % 2, :], ALU.add, ALU.mult
                ).then_inc(hT_done.sem, 1)
                dve.wait_ge(hT_done.sem, hT_done.at(this, f + 1))
                split(hT[:, f % 2, :], hT_hi[:, f, :], hT_lo[:, f, :], hT_hi_done, hT_split, this, f + 1)

            def residual2(this, t):
                dve.wait_ge(f2_done.sem, f2_done.at(this, t + 1))
                dve.wait_ge(x1_b2_done.sem, x1_b2_done.at(this, t + 1))
                dve.wait_ge(out_stored[t].sem, out_stored[t].at((this[0], this[1] - 1), 16))
                nc.vector.tensor_tensor(y2[:, t, :], main[:, t, 0:D], x1_b2[:, t, :], ALU.add).then_inc(y2_done.sem, 1)

            def residual3(this, t):
                dve.wait_ge(rstd2_done.sem, rstd2_done.at(this, t + 1))
                nc.vector.scalar_tensor_tensor(
                    y2[:, t, :], y2[:, t, :], stats[:, 1, 2:3], row("alpha2"), ALU.mult, ALU.mult
                ).then_inc(x2_done.sem, 1)
                dve.wait_ge(x2_done.sem, x2_done.at(this, t + 1))
                if t == 0:
                    dve.wait_ge(x_gamma2_done.sem, x_gamma2_done.at(this, 1))
                nc.vector.tensor_tensor(y2[:, t, :], y2[:, t, :], x_gamma2[:, t, :], ALU.add).then_inc(z_done.sem, 1)
                dve.wait_ge(z_done.sem, z_done.at(this, t + 1))
                nc.vector.bn_stats(bn[:, :], y2[:, t, :]).then_inc(bn_done.sem, 1)
                dve.wait_ge(consts_ready.sem, 1)
                dve.wait_ge(bn_done.sem, bn_done.at(this, t + 1))
                nc.vector.bn_aggr(moments[:, :], bn[:, :]).then_inc(moments_done.sem, 1)

            def layernorm(this, t):
                dve.wait_ge(rstd3_done.sem, rstd3_done.at(this, t + 1))
                nc.vector.tensor_scalar(
                    y2[:, t, :], y2[:, t, :], moments[:, 0:1], ln_stats[:, 1:2], ALU.subtract, ALU.mult
                ).then_inc(out_ready.sem, 1)

            def iteration(i, attention, ffn, following):
                this, att, nxt = (i, 0), (i, 1), (i, 2)
                if attention:
                    for t in range(TILES):
                        evacuate_v(att, t)
                for slot in range(SLOTS):
                    for t in range(TILES):
                        if attention and slot == SCORES_AT[t]:
                            bias_and_max(att, t)
                        if attention and slot == CTX_AT[t]:
                            normalize_context(att, t)
                        if attention and slot == CTXT_AT[t]:
                            context_lo(att, t)
                        if attention and slot == WO_AT[t]:
                            residual1(att, t)
                        if attention and slot == X1SPLIT_AT[t]:
                            split_x1T(att, t)
                    if ffn and slot < KF:
                        silu(this, slot)
                    if following and slot == XT_SPLIT_AT:
                        dve.wait_ge(v_done.sem, v_done.at(att, TILES))
                        split_xT(nxt)
                    if ffn and slot == KF + F2_PARTS - 1:
                        residual2(this, 0)
                    if ffn and slot == KF + F2_PARTS + 1:
                        residual3(this, 0)
                    if ffn and slot == KF + F2_PARTS + 3:
                        layernorm(this, 0)
                if ffn:
                    for t in range(1, TILES):
                        residual2(this, t)
                        residual3(this, t)
                        layernorm(this, t)

            split_xT((0, 0))
            for unit in range(UNITS):
                if unit == KD:
                    prepare_constants()
                dve.wait_ge(w_hi_done.sem, unit + 1)
                nc.vector.tensor_tensor(
                    w_lo[:, unit, :], stage[unit % 2][:, :], plain(w_hi[:, unit, :]), ALU.subtract
                ).then_inc(w_lo_done.sem, 1)
            all_iterations(dve, iteration)

        @block.gpsimd
        def _(pool):
            pool.sem_inc(x1_scaled.sem, TILES)

            def add_gamma2(this):
                pool.wait_ge(x_in.sem, x_in.at(this, 16))
                pool.wait_ge(z_done.sem, z_done.at((this[0], this[1] - 1), TILES))
                nc.gpsimd.tensor_tensor(
                    x_gamma2[:, :, :], x[:, :, :],
                    row("gamma2").unsqueeze(1).to_broadcast([P, TILES, D]), ALU.add,
                ).then_inc(x_gamma2_done.sem, 1)

            def add_bo(att):
                pool.wait_ge(x_in.sem, x_in.at(att, 16))
                pool.wait_ge(x1T_evacuated.sem, x1T_evacuated.at((att[0], att[1] - 1), TILES))
                pool.wait_ge(x1_scaled.sem, x1_scaled.at((att[0], att[1] - 1), TILES))
                nc.gpsimd.tensor_tensor(
                    y1[:, :, :], x[:, :, :],
                    row("bo").unsqueeze(1).to_broadcast([P, TILES, D]), ALU.add,
                ).then_inc(x_bo_done.sem, 1)

            def x1_and_b2(this, t):
                pool.wait_ge(y1_normalized.sem, y1_normalized.at(this, t + 1))
                pool.wait_ge(y2_done.sem, y2_done.at((this[0], this[1] - 1), t + 1))
                nc.gpsimd.tensor_tensor(x1_b2[:, t, :], y1[:, t, :], row("alpha1"), ALU.mult).then_inc(x1_scaled.sem, 1)
                pool.wait_ge(x1_scaled.sem, x1_scaled.at(this, t + 1))
                nc.gpsimd.tensor_tensor(x1_b2[:, t, :], x1_b2[:, t, :], row("b2"), ALU.add).then_inc(x1_b2_done.sem, 1)

            def inverse_rms(group, t, norm, squares_done, mean_done, rstd_done):
                pool.wait_ge(squares_done.sem, squares_done.at(group, t + 1))
                nc.gpsimd.tensor_tensor(
                    stats[:, norm, 1:2], stats[:, norm, 0:1], rms_eps[:, :], ALU.add
                ).then_inc(mean_done.sem, 1)
                pool.wait_ge(mean_done.sem, mean_done.at(group, t + 1))
                nc.gpsimd.tensor_tensor(stats[:, norm, 2:3], stats[:, norm, 1:2], minus_half[:, :], ALU.pow).then_inc(rstd_done.sem, 1)

            def inverse_deviation(this, t):
                pool.wait_ge(moments_done.sem, moments_done.at(this, t + 1))
                nc.gpsimd.tensor_tensor(ln_stats[:, 0:1], moments[:, 1:2], ln_eps[:, :], ALU.add).then_inc(var_done.sem, 1)
                pool.wait_ge(var_done.sem, var_done.at(this, t + 1))
                nc.gpsimd.tensor_tensor(ln_stats[:, 1:2], ln_stats[:, 0:1], minus_half[:, :], ALU.pow).then_inc(rstd3_done.sem, 1)

            def iteration(i, attention, ffn, following):
                this, att = (i, 0), (i, 1)
                if ffn:
                    add_gamma2(this)
                    for t in range(TILES):
                        x1_and_b2(this, t)
                if attention:
                    add_bo(att)
                    inverse_rms(att, 0, 0, squares1_done, mean1_done, rstd1_done)
                if ffn:
                    inverse_rms(this, 0, 1, squares2_done, mean2_done, rstd2_done)
                if attention:
                    inverse_rms(att, 1, 0, squares1_done, mean1_done, rstd1_done)
                if ffn:
                    inverse_deviation(this, 0)
                    inverse_rms(this, 1, 1, squares2_done, mean2_done, rstd2_done)
                    inverse_deviation(this, 1)

            pool.wait_ge(consts_ready.sem, 1)
            pool.wait_ge(w_lo_done.sem, UNITS)
            all_iterations(pool, iteration)


def kernel(**inputs):
    import numpy as np
    import concourse.bacc as bacc
    from concourse.bass_utils import run_bass_kernel_spmd

    given = {name.removeprefix("L0_gnn_"): np.asarray(a) for name, a in inputs.items()}
    x, adj = given["x"], given["adj"]
    B, N, D = x.shape
    G = B // TILES
    dh = D // HEADS
    kd = D // P
    spare = dh // kd

    order = []
    for c in range(kd):
        for odd in range(2):
            order += [(2 * c + odd) * dh + d for d in range(dh)]
            order += [(2 * kd + odd) * dh + c * spare + d for d in range(spare)]

    def by_chunk(a):
        return a.reshape(-1, P).T

    arrays = {
        "xT_in": x.reshape(G, TILES * N, kd, P).transpose(0, 3, 2, 1).reshape(G, P, kd * TILES * N),
        "x_in": x.reshape(G, TILES, N, D).transpose(0, 2, 1, 3).reshape(G, N, TILES * D),
        "adj_in": adj.reshape(G, TILES, N, N).transpose(0, 2, 1, 3).reshape(G, N, TILES * N),
        "watt_in": np.concatenate([given["wq"][:, order], given["wk"][:, order], given["wv"], given["wo"]], axis=1),
        "w1_in": given["w1"],
        "w2_in": given["w2"],
        "cols_in": np.concatenate(
            [by_chunk(given["bq"][order]), by_chunk(given["bk"][order]), by_chunk(given["b1"]),
             by_chunk(given["alpha1"]), by_chunk(given["gamma1"])], axis=1),
        "rows_in": np.broadcast_to(np.stack([given[n] for n in ROW_NAMES]), (P, len(ROW_NAMES), D)),
        "ident_in": np.eye(P, dtype=np.float32),
    }
    arrays = {name: np.ascontiguousarray(a) for name, a in arrays.items()}
    nc = bacc.Bacc("TRN2", target_bir_lowering=False, num_devices=1)
    args = [nc.dram_tensor(name, a.shape, mybir.dt.from_np(a.dtype), kind="ExternalInput").ap() for name, a in arrays.items()]
    out = nc.dram_tensor("out", (G, P, TILES * D), F32, kind="ExternalOutput").ap()
    build(nc, *args, out)
    result = run_bass_kernel_spmd(nc, [arrays], core_ids=[0]).results[0]["out"]
    return result.reshape(G, N, TILES, D).transpose(0, 2, 1, 3).reshape(B, N, D)
```

```python
from contextlib import ExitStack

import concourse.bass as bass
from concourse import mybir

P = 128
F32 = mybir.dt.float32
F32R = mybir.dt.float32r
ALU = mybir.AluOpType
ACT = mybir.ActivationFunctionType
AX_X = mybir.AxisListType.X

HEADS = 8
TILES = 2
RMS_EPS = 1e-6
LN_EPS = 1e-5

COL_NAMES = ("bq", "bk", "b1", "alpha1", "gamma1")
ROW_NAMES = ("bv", "bo", "alpha1", "gamma1", "b2", "alpha2", "gamma2")

QKV_AT = (0, 0, 1, 1, 2, 2, 3, 3)
SCORES_AT = (6, 12)
PT_AT = (10, 16)
CTX_AT = (10, 17)
CTXT_AT = (12, 18)
WO_AT = (13, 20)
X1T_AT = (16, 22)
EXP_AT = ((6, 7, 7, 8), (13, 14, 14, 14))
PT_HALF0_AT = (8, 16)
CTXT_HI_AT = (12, 18)
SQUARES1_AT = (14, 18)
Y1_NORMALIZED_AT = (15, 18)
X1T_EVACUATED_AT = (16, 21)
BIAS_AT = ((5, 5), (12, 13))
PT_HALF1_AT = (8, 14)
CONTEXT_AT = (9, 16)
CTXT_LO_AT = (12, 19)
Y1_AT = (13, 21)
X1T_SPLIT_AT = (16, 23)
XT_SPLIT_AT = 9
Y2_AFTER = 0
SQUARES2_AFTER = 0
Z_AFTER = 2
LAYERNORM_AFTER = 5
ALONE_EARLIER = 2
W_SPLIT_AT = (4, 5, 6, 9, 12, 15)


class Signal:

    def __init__(self, sem, n, primed=False):
        self.sem, self.n, self.primed = sem, n, primed

    def at(self, group, event):
        i, offset = group
        return i * self.n + (offset + self.primed) * self.n + event


def build(nc, xT_d, x_d, adj_d, watt_d, w1_d, w2_d, cols_d, rows_d, ident_d, out_d):
    G = x_d.shape[0]
    D = watt_d.shape[0]
    FF = w1_d.shape[1]
    KD = D // P
    KF = FF // P
    DH = D // HEADS
    NT = TILES * P
    SCALE = float(DH) ** -0.5
    UNIT = 4 * D
    assert UNIT == FF and KF % 4 == 0
    UNITS = 2 * KD + KF // 4
    QK = 2 * KD
    F2_PARTS = KF // 2
    SLOTS = KF + TILES * F2_PARTS
    HALF = HEADS // 2
    RING = UNIT // (2 * NT)
    PAIRS = KD

    col_at, at = {}, 0
    for name in COL_NAMES:
        col_at[name] = at
        at += KF if name == "b1" else KD

    with ExitStack() as ctx:

        def sb(name, shape, dt=F32):
            return ctx.enter_context(nc.sbuf_tensor(name, shape, dt))

        def ps(name, shape):
            return ctx.enter_context(nc.psum_tensor(name, shape, F32))

        def signal(name, n, primed=False):
            return Signal(ctx.enter_context(nc.semaphore(name)), n, primed)

        w_hi = sb("w_hi", [P, UNITS, UNIT], F32R)
        w_lo = sb("w_lo", [P, UNITS, UNIT], F32R)
        cols = sb("cols", [P, at])
        cols_scaled = sb("cols_scaled", [P, KD + KF])
        rows = sb("rows", [P, len(ROW_NAMES), D])
        ident = sb("ident", [P, P])
        minus_half = sb("minus_half", [P, 1])
        rms_eps = sb("rms_eps", [P, 1])
        ln_eps = sb("ln_eps", [P, 1])

        STAGES = 2 * KF * NT // UNIT + 2
        with nc.sbuf_tensor("stage", [P, STAGES, UNIT], F32) as stage:
            pass
        hT_hi = sb("hT_hi", [P, KF, NT], F32R)
        hT_lo = sb("hT_lo", [P, KF, NT], F32R)
        ffn_scratch = sb("ffn_scratch", [P, UNIT])
        tail_scratch = sb("tail_scratch", [P, UNIT])
        half_z = ffn_scratch[:, 0 : RING * NT].rearrange("p (r n) -> p r n", r=RING)
        hT = ffn_scratch[:, RING * NT : 2 * RING * NT].rearrange("p (r n) -> p r n", r=RING)
        x1_b2 = tail_scratch[:, 0 : TILES * D].rearrange("p (t n) -> p t n", t=TILES)
        y2 = tail_scratch[:, TILES * D : 2 * TILES * D].rearrange("p (t n) -> p t n", t=TILES)

        xT = sb("xT", [P, KD, NT])
        xT_hi = sb("xT_hi", [P, KD, NT], F32R)
        xT_lo = sb("xT_lo", [P, KD, NT], F32R)
        x = sb("x", [P, TILES, D])
        x_gamma2 = sb("x_gamma2", [P, TILES, D])
        adj = sb("adj", [P, TILES, P])
        qkT = sb("qkT", [P, QK, NT])
        qkT_last = sb("qkT_last", [P, 2, NT])
        v = sb("v", [P, TILES, HEADS, DH + 1])
        probs = sb("probs", [P, HEADS, P])
        probsT = sb("probsT", [P, HEADS, P])
        neg_max = sb("neg_max", [P, HEADS])
        inv_sum = sb("inv_sum", [P, HEADS])
        context = sb("context", [P, D])
        ctxT_hi = sb("ctxT_hi", [P, KD, P], F32R)
        ctxT_lo = sb("ctxT_lo", [P, KD, P], F32R)
        y1 = sb("y1", [P, TILES, D])
        x1T = sb("x1T", [P, KD, P])
        x1T_hi = sb("x1T_hi", [P, KD, NT], F32R)
        x1T_lo = sb("x1T_lo", [P, KD, NT], F32R)
        squares1_out = sb("squares1_out", [P, D], mybir.dt.bfloat16)
        squares2_out = sb("squares2_out", [P, D], mybir.dt.bfloat16)
        stats = sb("stats", [P, 2, 3])
        bn = sb("bn", [P, 6])
        moments = sb("moments", [P, 2])
        ln_stats = sb("ln_stats", [P, 2])

        main = ps("main", [P, 2, 512])
        scores = ps("scores", [P, HEADS * P])
        probsT_ps = ps("probsT_ps", [P, HEADS * P])
        small = ps("small", [P, 2, 512])

        weights_in = [signal(f"weights_in{n}", 0) for n in range(STAGES)]
        consts_in = signal("consts_in", 0)
        rows_in = signal("rows_in", 0)
        xT_in = signal("xT_in", 16)
        x_in = signal("x_in", 16)
        adj_in = signal("adj_in", 16)
        heads_moved = signal("heads_moved", 16 * 2 * PAIRS)
        out_stored = [signal(f"out_stored{t}", 16, primed=True) for t in range(TILES)]
        w_hi_done = signal("w_hi_done", 0)
        watt_lo_done = signal("watt_lo_done", 0)
        w12_lo_done = signal("w12_lo_done", 0)
        consts_ready = signal("consts_ready", 0)
        qk_done = signal("qk_done", QK)
        v_done = signal("v_done", TILES)
        scores_done = signal("scores_done", TILES)
        pt_done = signal("pt_done", TILES)
        ctx_done = signal("ctx_done", TILES)
        ctxT_done = signal("ctxT_done", TILES)
        wo_done = signal("wo_done", TILES)
        x1T_done = signal("x1T_done", TILES)
        f1_done = signal("f1_done", KF)
        f2_done = signal("f2_done", TILES)
        qk_evacuated = signal("qk_evacuated", QK)
        exp_done = signal("exp_done", TILES)
        pt_evacuated0 = signal("pt_evacuated0", TILES)
        ctxT_hi_done = signal("ctxT_hi_done", TILES)
        squares1_done = signal("squares1_done", TILES)
        y1_normalized = signal("y1_normalized", TILES)
        x1T_evacuated = signal("x1T_evacuated", TILES, primed=True)
        half_z_done = signal("half_z_done", KF)
        tanh_done = signal("tanh_done", KF)
        squares2_done = signal("squares2_done", TILES)
        xT_hi_done = signal("xT_hi_done", 1)
        xT_split = signal("xT_split", 1)
        v_evacuated = signal("v_evacuated", TILES)
        scores_biased = signal("scores_biased", 2 * TILES, primed=True)
        max_done = signal("max_done", 2 * TILES)
        pt_evacuated1 = signal("pt_evacuated1", TILES)
        inv_sum_done = signal("inv_sum_done", TILES)
        context_done = signal("context_done", TILES)
        ctxT_lo_done = signal("ctxT_lo_done", TILES)
        y1_done = signal("y1_done", TILES, primed=True)
        x1T_hi_done = signal("x1T_hi_done", TILES)
        x1T_split = signal("x1T_split", TILES, primed=True)
        hT_done = signal("hT_done", KF)
        hT_hi_done = signal("hT_hi_done", KF)
        hT_split = signal("hT_split", KF, primed=True)
        y2_done = signal("y2_done", TILES, primed=True)
        x2_done = signal("x2_done", TILES)
        z_done = signal("z_done", TILES, primed=True)
        bn_done = signal("bn_done", TILES)
        moments_done = signal("moments_done", TILES)
        out_ready = signal("out_ready", TILES)
        b2_gamma1_done = signal("b2_gamma1_done", 0)
        x_gamma2_done = signal("x_gamma2_done", 1)
        x_bo_done = signal("x_bo_done", 1)
        x1_scaled = signal("x1_scaled", TILES, primed=True)
        x1_b2_done = signal("x1_b2_done", TILES)
        mean1_done = signal("mean1_done", TILES)
        rstd1_done = signal("rstd1_done", TILES)
        mean2_done = signal("mean2_done", TILES)
        rstd2_done = signal("rstd2_done", TILES)
        var_done = signal("var_done", TILES)
        rstd3_done = signal("rstd3_done", TILES)

        def main_tiles(attention, ffn):
            tiles = []
            for slot in range(SLOTS):
                if attention:
                    for n in range(QK + TILES):
                        if QKV_AT[n] == slot:
                            tiles.append(("qk", n) if n < QK else ("v", n - QK))
                if ffn and slot < KF:
                    tiles.append(("up", slot))
                if ffn and slot >= KF and (slot - KF) % F2_PARTS == 0:
                    tiles.append(("down", (slot - KF) // F2_PARTS))
            assert len(tiles) % 2 == 0
            return tiles

        def tail_steps(i, slot, ffn, tail, after):
            steps = []
            for t in range(TILES):
                at = KF + (t + 1) * F2_PARTS - 1 + after
                if ffn and slot == at:
                    steps.append((t, (i, 0)))
                if tail and slot == at - SLOTS:
                    steps.append((t, (i, -1)))
            return steps

        def batch_slots(slot, ffn):
            return (slot, slot if ffn else slot + ALONE_EARLIER)

        def bank(kind, n, attention, ffn):
            return main[:, main_tiles(attention, ffn).index((kind, n)) % 2, :]

        def row(name):
            return rows[:, ROW_NAMES.index(name), :]

        def col(name, c):
            return cols[:, col_at[name] + c : col_at[name] + c + 1]

        def plain(ap):
            return ap.bitcast(F32)

        def tokens(t):
            return slice(t * P, (t + 1) * P)

        def dram_group(ap, group):
            i, offset = group
            return ap[bass.ds(i + offset, 1), :, :].rearrange("g p n -> (g p) n")

        def weight_source(unit):
            if unit < KD:
                return watt_d[unit * P : (unit + 1) * P, :]
            if unit < 2 * KD:
                return w1_d[(unit - KD) * P : (unit - KD + 1) * P, :]
            first = (unit - 2 * KD) * 4 * P
            return w2_d[first : first + 4 * P, :].rearrange("(f p) n -> p f n", p=P)

        def w2_cols(f):
            return 2 * KD + f // 4, slice((f % 4) * D, (f % 4 + 1) * D)

        def all_iterations(engine, iteration):
            iteration(-1, True, True, False, False)
            iteration(0, True, True, True, False)
            with engine.Fori(1, G - 2) as i:
                iteration(i, True, True, True, True)
            iteration(G - 2, False, True, True, True)
            iteration(G - 1, False, False, True, True)
            iteration(G, False, False, False, True)

        block = ctx.enter_context(nc.Block())

        @block.sync
        def _(sp):
            for t in range(TILES):
                sp.sem_inc(out_stored[t].sem, 16)
            sp.dma_start(xT[:, :, :], dram_group(xT_d, (0, 0)).rearrange("p (k n) -> p k n", k=KD)).then_inc(xT_in.sem, 16)

            def load_weights(unit):
                dst = stage[:, unit % STAGES, :]
                if unit >= 2 * KD:
                    dst = dst.rearrange("p (f n) -> p f n", f=4)
                sp.dma_start(dst, weight_source(unit)).then_inc(weights_in[unit % STAGES].sem, 16)

            sp.dma_start(cols[:, :], cols_d).then_inc(consts_in.sem, 16)
            sp.dma_start(ident[:, :], ident_d).then_inc(consts_in.sem, 16)
            for unit in range(KD):
                load_weights(unit)
            sp.dma_start(rows[:, :, :], rows_d).then_inc(rows_in.sem, 16)

            def store(group, t):
                sp.wait_ge(out_ready.sem, out_ready.at(group, t + 1))
                sp.dma_start(
                    dram_group(out_d, group)[:, t * D : (t + 1) * D], y2[:, t, :]
                ).then_inc(out_stored[t].sem, 16)

            def iteration(i, following, attention, ffn, tail):
                before, this, att, nxt = (i, -1), (i, 0), (i, 1), (i, 2)
                if attention:
                    if ffn:
                        sp.wait_ge(scores_biased.sem, scores_biased.at(this, 2 * TILES))
                    sp.dma_start(adj[:, :, :], dram_group(adj_d, att).rearrange("p (t n) -> p t n", t=TILES)).then_inc(adj_in.sem, 16)
                if following:
                    sp.wait_ge(xT_split.sem, xT_split.at(att, 1))
                    sp.dma_start(xT[:, :, :], dram_group(xT_d, nxt).rearrange("p (k n) -> p k n", k=KD)).then_inc(xT_in.sem, 16)
                if attention and not ffn:
                    for unit in range(KD, STAGES):
                        load_weights(unit)
                if attention:
                    spare = DH // PAIRS
                    for c in range(PAIRS):
                        sp.wait_ge(qk_evacuated.sem, qk_evacuated.at(att, 2 * c + 2))
                        for half in (0, 64):
                            sp.dma_start(
                                qkT_last[half + c * spare : half + (c + 1) * spare, :, :],
                                qkT[half + DH : half + DH + spare, 2 * c : 2 * c + 2, :],
                            ).then_inc(heads_moved.sem, 16)
                if attention and not ffn:
                    for unit in range(STAGES, UNITS):
                        sp.wait_ge(watt_lo_done.sem, unit - STAGES + 1)
                        load_weights(unit)
                if tail:
                    store(before, 1)
                if attention:
                    if ffn:
                        sp.wait_ge(x_gamma2_done.sem, x_gamma2_done.at(this, 1))
                    sp.dma_start(x[:, :, :], dram_group(x_d, att).rearrange("p (t n) -> p t n", t=TILES)).then_inc(x_in.sem, 16)
                if ffn:
                    store(this, 0)

            all_iterations(sp, iteration)
            for t in range(TILES):
                sp.wait_ge(out_stored[t].sem, out_stored[t].at((G - 1, 0), 16))

        @block.tensor
        def _(pe):
            HI_LO = ((0, 0), (0, 1), (1, 0))

            def product(out, left, right, steps, first, last):
                for n, step in enumerate(steps):
                    for m, (a, b) in enumerate(HI_LO):
                        done = nc.tensor.matmul(
                            out,
                            left[a](step),
                            right[b](step),
                            start=first and n == 0 and m == 0,
                            stop=last and n == len(steps) - 1 and m == 2,
                        )
                return done

            def free_bank(i, kind, n, attention, ffn, tail):
                before, this, att = (i, -1), (i, 0), (i, 1)
                tiles = main_tiles(attention, ffn)
                at = tiles.index((kind, n))
                if at < 2:
                    if ffn and attention:
                        pe.wait_ge(v_evacuated.sem, v_evacuated.at(this, at + 1))
                    if tail or ffn:
                        pe.wait_ge(y2_done.sem, y2_done.at(before, at + 1))
                    return
                kind, n = tiles[at - 2]
                if kind == "qk":
                    pe.wait_ge(qk_evacuated.sem, qk_evacuated.at(att, n + 1))
                if kind == "v":
                    pe.wait_ge(v_evacuated.sem, v_evacuated.at(att, n + 1))
                if kind == "up":
                    pe.wait_ge(half_z_done.sem, half_z_done.at(this, n + 1))
                if kind == "down":
                    pe.wait_ge(y2_done.sem, y2_done.at(this, n + 1))

            def project_qk(att, n, out):
                if n == 0:
                    pe.wait_ge(xT_split.sem, xT_split.at(att, 1))
                product(
                    out[:, 0:NT],
                    [lambda k, w=w: w[:, k, tokens(n)] for w in (w_hi, w_lo)],
                    [lambda k, a=a: a[:, k, :] for a in (xT_hi, xT_lo)],
                    range(KD), True, True,
                ).then_inc(qk_done.sem, 1)

            def project_v(att, t, out):
                product(
                    out[:, 0:D],
                    [lambda k, a=a: a[:, k, tokens(t)] for a in (xT_hi, xT_lo)],
                    [lambda k, w=w: w[:, k, 2 * D : 3 * D] for w in (w_hi, w_lo)],
                    range(KD), True, True,
                ).then_inc(v_done.sem, 1)

            def score_step(att, t):
                if t == 0:
                    pe.wait_ge(qk_evacuated.sem, qk_evacuated.at(att, QK))
                    pe.wait_ge(heads_moved.sem, heads_moved.at(att, heads_moved.n))
                if t == 0:
                    pe.wait_ge(scores_biased.sem, scores_biased.at((att[0], att[1] - 1), 2 * TILES))
                else:
                    pe.wait_ge(scores_biased.sem, scores_biased.at(att, 2 * t))
                for h in range(HEADS):
                    c, odd = divmod(h, 2)
                    at = slice(64 * odd, 64 * odd + DH)
                    if c < PAIRS:
                        q, k = qkT[at, 2 * c, tokens(t)], qkT[at, 2 * c + 1, tokens(t)]
                    else:
                        q, k = qkT_last[at, 0, tokens(t)], qkT_last[at, 1, tokens(t)]
                    j = odd * HALF + c
                    done = nc.tensor.matmul(scores[:, tokens(j)], q, k, start=True, stop=True)
                done.then_inc(scores_done.sem, 1)

            def transpose_probs(att, t):
                pe.wait_ge(exp_done.sem, exp_done.at(att, t + 1))
                for j in range(HEADS):
                    done = nc.tensor.transpose(probsT_ps[:, tokens(j)], probs[:, j, :], ident[:, :])
                done.then_inc(pt_done.sem, 1)

            def context_step(att, t):
                pe.wait_ge(pt_evacuated0.sem, pt_evacuated0.at(att, t + 1))
                pe.wait_ge(pt_evacuated1.sem, pt_evacuated1.at(att, t + 1))
                if t == 0:
                    pe.wait_ge(v_evacuated.sem, v_evacuated.at(att, TILES))
                    pe.wait_ge(y1_done.sem, y1_done.at((att[0], att[1] - 1), TILES))
                else:
                    pe.wait_ge(y1_done.sem, y1_done.at(att, t))
                for h in range(HEADS):
                    j = (h % 2) * HALF + h // 2
                    done = nc.tensor.matmul(
                        small[:, 0, h * (DH + 1) : (h + 1) * (DH + 1)],
                        probsT[:, j, :], v[:, t, h, :], start=True, stop=True,
                    )
                done.then_inc(ctx_done.sem, 1)

            def transpose_context(att, t):
                pe.wait_ge(context_done.sem, context_done.at(att, t + 1))
                if t == 0:
                    pe.wait_ge(x1T_evacuated.sem, x1T_evacuated.at((att[0], att[1] - 1), TILES))
                else:
                    pe.wait_ge(x1T_evacuated.sem, x1T_evacuated.at(att, t))
                for c in range(KD):
                    done = nc.tensor.transpose(small[:, 1, tokens(c)], context[:, tokens(c)], ident[:, :])
                done.then_inc(ctxT_done.sem, 1)

            def output_projection(att, t):
                pe.wait_ge(ctxT_lo_done.sem, ctxT_lo_done.at(att, t + 1))
                product(
                    small[:, 0, 0:D],
                    [lambda k, a=a: a[:, k, :] for a in (ctxT_hi, ctxT_lo)],
                    [lambda k, w=w: w[:, k, 3 * D : 4 * D] for w in (w_hi, w_lo)],
                    range(KD), True, True,
                ).then_inc(wo_done.sem, 1)

            def transpose_x1(att, t):
                pe.wait_ge(y1_normalized.sem, y1_normalized.at(att, t + 1))
                for c in range(KD):
                    done = nc.tensor.transpose(small[:, 1, tokens(c)], y1[:, t, tokens(c)], ident[:, :])
                done.then_inc(x1T_done.sem, 1)

            def ffn_up(this, f, out):
                if f == 0:
                    pe.wait_ge(x1T_split.sem, x1T_split.at(this, TILES))
                product(
                    out[:, 0:NT],
                    [lambda k, w=w: w[:, KD + k, tokens(f)] for w in (w_hi, w_lo)],
                    [lambda k, a=a: a[:, k, :] for a in (x1T_hi, x1T_lo)],
                    range(KD), True, True,
                ).then_inc(f1_done.sem, 1)

            def ffn_down(this, t, part, out):
                if t == 0:
                    pe.wait_ge(hT_split.sem, hT_split.at(this, 2 * part + 2))
                last = part == F2_PARTS - 1
                done = product(
                    out[:, 0:D],
                    [lambda f, a=a: a[:, f, tokens(t)] for a in (hT_hi, hT_lo)],
                    [lambda f, w=w: w[:, w2_cols(f)[0], w2_cols(f)[1]] for w in (w_hi, w_lo)],
                    (2 * part, 2 * part + 1), part == 0, last,
                )
                if last:
                    done.then_inc(f2_done.sem, 1)

            def iteration(i, following, attention, ffn, tail):
                this, att = (i, 0), (i, 1)
                for slot in range(SLOTS if attention or ffn else 0):
                    at = batch_slots(slot, ffn)
                    for n in range(QK + TILES):
                        if attention and slot == QKV_AT[n] and n < QK:
                            free_bank(i, "qk", n, attention, ffn, tail)
                            project_qk(att, n, bank("qk", n, attention, ffn))
                        elif attention and slot == QKV_AT[n]:
                            free_bank(i, "v", n - QK, attention, ffn, tail)
                            project_v(att, n - QK, bank("v", n - QK, attention, ffn))
                    for t in range(TILES):
                        if attention and at[t] == SCORES_AT[t]:
                            score_step(att, t)
                        if attention and at[t] == PT_AT[t]:
                            transpose_probs(att, t)
                        if attention and at[t] == CTX_AT[t]:
                            context_step(att, t)
                        if attention and at[t] == CTXT_AT[t]:
                            transpose_context(att, t)
                        if attention and at[t] == WO_AT[t]:
                            output_projection(att, t)
                        if attention and at[t] == X1T_AT[t]:
                            transpose_x1(att, t)
                    if ffn and not tail and slot == 0:
                        pe.wait_ge(w12_lo_done.sem, UNITS - KD)
                    if ffn and slot < KF:
                        free_bank(i, "up", slot, attention, ffn, tail)
                        ffn_up(this, slot, bank("up", slot, attention, ffn))
                    if ffn and slot >= KF:
                        t, part = divmod(slot - KF, F2_PARTS)
                        if part == 0:
                            free_bank(i, "down", t, attention, ffn, tail)
                        ffn_down(this, t, part, bank("down", t, attention, ffn))

            pe.wait_ge(watt_lo_done.sem, KD)
            pe.wait_ge(consts_ready.sem, 1)
            iteration(-1, True, True, False, False)
            iteration(0, True, True, True, False)
            with pe.Fori(1, G - 2) as i:
                iteration(i, True, True, True, True)
            iteration(G - 2, False, True, True, True)
            iteration(G - 1, False, False, True, True)

        @block.scalar
        def _(act):
            act.sem_inc(x1T_evacuated.sem, TILES)

            def split_hi(unit):
                act.wait_ge(weights_in[unit % STAGES].sem, 16 * (unit // STAGES + 1))
                nc.scalar.copy(w_hi[:, unit, :], stage[:, unit % STAGES, :]).then_inc(w_hi_done.sem, 1)

            def evacuate_qk(att, n, source):
                act.wait_ge(qk_done.sem, qk_done.at(att, n + 1))
                c = n // 2
                if n % 2 == 0:
                    bias, scale = cols_scaled[:, c : c + 1], SCALE
                else:
                    bias, scale = col("bk", c), 1.0
                nc.scalar.activation(qkT[:, n, :], source[:, 0:NT], ACT.Identity, bias=bias, scale=scale).then_inc(qk_evacuated.sem, 1)

            def exponentials(att, t, quarter):
                act.wait_ge(max_done.sem, max_done.at(att, 2 * t + quarter // 2 + 1))
                for j in range(quarter * HEADS // 4, (quarter + 1) * HEADS // 4):
                    done = nc.scalar.activation(probs[:, j, :], probs[:, j, :], ACT.Exp, bias=neg_max[:, j : j + 1])
                if quarter == 3:
                    done.then_inc(exp_done.sem, 1)

            def evacuate_probsT(att, t):
                act.wait_ge(pt_done.sem, pt_done.at(att, t + 1))
                nc.scalar.copy(probsT[:, 0:HALF, :], probsT_ps[:, 0 : HALF * P].rearrange("p (j n) -> p j n", j=HALF)).then_inc(pt_evacuated0.sem, 1)

            def context_hi(att, t):
                act.wait_ge(ctxT_done.sem, ctxT_done.at(att, t + 1))
                nc.scalar.copy(ctxT_hi[:, :, :], small[:, 1, 0:D].rearrange("p (c n) -> p c n", c=KD)).then_inc(ctxT_hi_done.sem, 1)

            def squares1(att, t):
                act.wait_ge(y1_done.sem, y1_done.at(att, t + 1))
                nc.scalar.activation(squares1_out[:, :], y1[:, t, :], ACT.Square, scale=D**-0.5, accum_out=stats[:, 0, 0:1]).then_inc(squares1_done.sem, 1)

            def normalize1(att, t):
                act.wait_ge(rstd1_done.sem, rstd1_done.at(att, t + 1))
                nc.scalar.activation(y1[:, t, :], y1[:, t, :], ACT.Copy, scale=stats[:, 0, 2:3]).then_inc(y1_normalized.sem, 1)

            def evacuate_x1T(att, t):
                act.wait_ge(x1T_done.sem, x1T_done.at(att, t + 1))
                if t == 0:
                    act.wait_ge(x1T_split.sem, x1T_split.at((att[0], att[1] - 1), TILES))
                else:
                    act.wait_ge(x1T_split.sem, x1T_split.at(att, t))
                for c in range(KD):
                    done = nc.scalar.activation(x1T[:, c, :], small[:, 1, tokens(c)], ACT.Identity, bias=col("gamma1", c), scale=col("alpha1", c))
                done.then_inc(x1T_evacuated.sem, 1)

            def silu_parts(this, f, source):
                act.wait_ge(f1_done.sem, f1_done.at(this, f + 1))
                if f >= RING:
                    act.wait_ge(hT_split.sem, hT_split.at(this, f - RING + 1))
                else:
                    act.wait_ge(hT_split.sem, hT_split.at((this[0], this[1] - 1), KF - RING + f + 1))
                nc.scalar.activation(half_z[:, f % RING, :], source[:, 0:NT], ACT.Identity, bias=cols_scaled[:, KD + f : KD + f + 1], scale=0.5).then_inc(half_z_done.sem, 1)
                act.wait_ge(half_z_done.sem, half_z_done.at(this, f + 1))
                nc.scalar.activation(hT[:, f % RING, :], half_z[:, f % RING, :], ACT.Tanh).then_inc(tanh_done.sem, 1)

            def squares2(this, t):
                act.wait_ge(y2_done.sem, y2_done.at(this, t + 1))
                nc.scalar.activation(squares2_out[:, :], y2[:, t, :], ACT.Square, scale=D**-0.5, accum_out=stats[:, 1, 0:1]).then_inc(squares2_done.sem, 1)

            def iteration(i, following, attention, ffn, tail):
                this, att = (i, 0), (i, 1)
                for slot in range(SLOTS):
                    at = batch_slots(slot, ffn)
                    if attention and not ffn and slot in W_SPLIT_AT:
                        split_hi(KD + W_SPLIT_AT.index(slot))
                    for n in range(QK):
                        if attention and slot == QKV_AT[n]:
                            evacuate_qk(att, n, bank("qk", n, attention, ffn))
                    for t in range(TILES):
                        for quarter in range(4):
                            if attention and at[t] == EXP_AT[t][quarter]:
                                exponentials(att, t, quarter)
                        if attention and at[t] == PT_HALF0_AT[t]:
                            evacuate_probsT(att, t)
                        if attention and at[t] == CTXT_HI_AT[t]:
                            context_hi(att, t)
                        if attention and at[t] == SQUARES1_AT[t]:
                            squares1(att, t)
                        if attention and at[t] == Y1_NORMALIZED_AT[t]:
                            normalize1(att, t)
                        if attention and at[t] == X1T_EVACUATED_AT[t]:
                            evacuate_x1T(att, t)
                    if ffn and slot < KF:
                        silu_parts(this, slot, bank("up", slot, attention, ffn))
                    for t, group in tail_steps(i, slot, ffn, tail, SQUARES2_AFTER):
                        squares2(group, t)

            for unit in range(KD):
                split_hi(unit)
            act.wait_ge(consts_ready.sem, 1)
            all_iterations(act, iteration)

        @block.vector
        def _(dve):
            for s in (scores_biased, y1_done, x1T_split, hT_split, y2_done, z_done):
                dve.sem_inc(s.sem, s.n)

            def split(source, hi, lo, hi_done, lo_done, group, event):
                nc.vector.tensor_copy(hi, source).then_inc(hi_done.sem, 1)
                dve.wait_ge(hi_done.sem, hi_done.at(group, event))
                nc.vector.tensor_tensor(lo, source, plain(hi), ALU.subtract).then_inc(lo_done.sem, 1)

            def split_xT(group):
                dve.wait_ge(xT_in.sem, xT_in.at(group, 16))
                split(xT[:, :, :], xT_hi[:, :, :], xT_lo[:, :, :], xT_hi_done, xT_split, group, 1)

            def prepare_constants():
                dve.wait_ge(consts_in.sem, 32)
                nc.vector.tensor_scalar(cols_scaled[:, 0:KD], cols[:, 0:KD], SCALE, None, ALU.mult)
                nc.vector.tensor_scalar(cols_scaled[:, KD:], cols[:, col_at["b1"] : col_at["b1"] + KF], 0.5, None, ALU.mult)
                nc.vector.memset(v[:, :, :, DH : DH + 1], 1.0)
                nc.vector.memset(minus_half[:, :], -0.5)
                nc.vector.memset(rms_eps[:, :], RMS_EPS)
                nc.vector.memset(ln_eps[:, :], LN_EPS).then_inc(consts_ready.sem, 1)

            def evacuate_v(att, t, source):
                dve.wait_ge(v_done.sem, v_done.at(att, t + 1))
                nc.vector.tensor_tensor(
                    v[:, t, :, 0:DH],
                    source[:, 0:D].rearrange("p (h d) -> p h d", h=HEADS),
                    row("bv").rearrange("p (h d) -> p h d", h=HEADS), ALU.add,
                ).then_inc(v_evacuated.sem, 1)

            def bias_and_max(att, t, half):
                heads = slice(half * HALF, (half + 1) * HALF)
                dve.wait_ge(scores_done.sem, scores_done.at(att, t + 1))
                if t == 0 and half == 0:
                    dve.wait_ge(adj_in.sem, adj_in.at(att, 16))
                nc.vector.tensor_tensor(
                    probs[:, heads, :],
                    scores[:, half * HALF * P : (half + 1) * HALF * P].rearrange("p (j n) -> p j n", j=HALF),
                    adj[:, t : t + 1, :].to_broadcast([P, HALF, P]), ALU.add,
                ).then_inc(scores_biased.sem, 1)
                dve.wait_ge(scores_biased.sem, scores_biased.at(att, 2 * t + half + 1))
                nc.vector.tensor_reduce(neg_max[:, heads], probs[:, heads, :], AX_X, ALU.max, negate=True).then_inc(max_done.sem, 1)

            def evacuate_probsT(att, t):
                dve.wait_ge(pt_done.sem, pt_done.at(att, t + 1))
                nc.vector.tensor_copy(
                    probsT[:, HALF:HEADS, :], probsT_ps[:, HALF * P : HEADS * P].rearrange("p (j n) -> p j n", j=HALF)
                ).then_inc(pt_evacuated1.sem, 1)

            def normalize_context(att, t):
                dve.wait_ge(ctx_done.sem, ctx_done.at(att, t + 1))
                sums = small[:, 0, 0 : HEADS * (DH + 1)].rearrange("p (h d) -> p h d", h=HEADS)
                nc.vector.reciprocal(inv_sum[:, :], sums[:, :, DH : DH + 1].rearrange("p h o -> p (h o)")).then_inc(inv_sum_done.sem, 1)
                dve.wait_ge(inv_sum_done.sem, inv_sum_done.at(att, t + 1))
                nc.vector.tensor_tensor(
                    context[:, :].rearrange("p (h d) -> p h d", h=HEADS),
                    sums[:, :, 0:DH],
                    inv_sum[:, :].unsqueeze(2).to_broadcast([P, HEADS, DH]), ALU.mult,
                ).then_inc(context_done.sem, 1)

            def context_lo(att, t):
                dve.wait_ge(ctxT_hi_done.sem, ctxT_hi_done.at(att, t + 1))
                nc.vector.tensor_tensor(
                    ctxT_lo[:, :, :], small[:, 1, 0:D].rearrange("p (c n) -> p c n", c=KD),
                    plain(ctxT_hi[:, :, :]), ALU.subtract,
                ).then_inc(ctxT_lo_done.sem, 1)

            def residual1(att, t):
                dve.wait_ge(wo_done.sem, wo_done.at(att, t + 1))
                if t == 0:
                    dve.wait_ge(x_bo_done.sem, x_bo_done.at(att, 1))
                nc.vector.tensor_tensor(y1[:, t, :], small[:, 0, 0:D], y1[:, t, :], ALU.add).then_inc(y1_done.sem, 1)

            def split_x1T(att, t):
                dve.wait_ge(x1T_evacuated.sem, x1T_evacuated.at(att, t + 1))
                split(x1T[:, :, :], x1T_hi[:, :, tokens(t)], x1T_lo[:, :, tokens(t)], x1T_hi_done, x1T_split, att, t + 1)

            def silu(this, f):
                if f < KF:
                    dve.wait_ge(tanh_done.sem, tanh_done.at(this, f + 1))
                    nc.vector.scalar_tensor_tensor(
                        hT[:, f % RING, :], hT[:, f % RING, :], 1.0, half_z[:, f % RING, :], ALU.add, ALU.mult
                    ).then_inc(hT_done.sem, 1)
                if f > 0:
                    dve.wait_ge(hT_hi_done.sem, hT_hi_done.at(this, f))
                    nc.vector.tensor_tensor(
                        hT_lo[:, f - 1, :], hT[:, (f - 1) % RING, :], plain(hT_hi[:, f - 1, :]), ALU.subtract
                    ).then_inc(hT_split.sem, 1)
                if f < KF:
                    dve.wait_ge(hT_done.sem, hT_done.at(this, f + 1))
                    nc.vector.tensor_copy(hT_hi[:, f, :], hT[:, f % RING, :]).then_inc(hT_hi_done.sem, 1)

            def residual2(this, t):
                dve.wait_ge(f2_done.sem, f2_done.at(this, t + 1))
                dve.wait_ge(x1_b2_done.sem, x1_b2_done.at(this, t + 1))
                dve.wait_ge(out_stored[t].sem, out_stored[t].at((this[0], this[1] - 1), 16))
                nc.vector.tensor_tensor(y2[:, t, :], main[:, t, 0:D], x1_b2[:, t, :], ALU.add).then_inc(y2_done.sem, 1)

            def residual3(this, t):
                dve.wait_ge(rstd2_done.sem, rstd2_done.at(this, t + 1))
                nc.vector.scalar_tensor_tensor(
                    y2[:, t, :], y2[:, t, :], stats[:, 1, 2:3], row("alpha2"), ALU.mult, ALU.mult
                ).then_inc(x2_done.sem, 1)
                dve.wait_ge(x2_done.sem, x2_done.at(this, t + 1))
                if t == 0:
                    dve.wait_ge(x_gamma2_done.sem, x_gamma2_done.at(this, 1))
                nc.vector.tensor_tensor(y2[:, t, :], y2[:, t, :], x_gamma2[:, t, :], ALU.add).then_inc(z_done.sem, 1)
                dve.wait_ge(z_done.sem, z_done.at(this, t + 1))
                nc.vector.bn_stats(bn[:, :], y2[:, t, :]).then_inc(bn_done.sem, 1)
                dve.wait_ge(consts_ready.sem, 1)
                dve.wait_ge(bn_done.sem, bn_done.at(this, t + 1))
                nc.vector.bn_aggr(moments[:, :], bn[:, :]).then_inc(moments_done.sem, 1)

            def layernorm(this, t):
                dve.wait_ge(rstd3_done.sem, rstd3_done.at(this, t + 1))
                nc.vector.tensor_scalar(
                    y2[:, t, :], y2[:, t, :], moments[:, 0:1], ln_stats[:, 1:2], ALU.subtract, ALU.mult
                ).then_inc(out_ready.sem, 1)

            def iteration(i, following, attention, ffn, tail):
                before, this, att, nxt = (i, -1), (i, 0), (i, 1), (i, 2)
                for slot in range(SLOTS):
                    at = batch_slots(slot, ffn)
                    for t in range(TILES):
                        if attention and slot == QKV_AT[QK + t]:
                            if t == 0 and not ffn:
                                dve.wait_ge(rows_in.sem, 16)
                            evacuate_v(att, t, bank("v", t, attention, ffn))
                        for half in range(2):
                            if attention and at[t] == BIAS_AT[t][half]:
                                bias_and_max(att, t, half)
                        if attention and at[t] == PT_HALF1_AT[t]:
                            evacuate_probsT(att, t)
                        if attention and at[t] == CONTEXT_AT[t]:
                            normalize_context(att, t)
                        if attention and at[t] == CTXT_LO_AT[t]:
                            context_lo(att, t)
                        if attention and at[t] == Y1_AT[t]:
                            residual1(att, t)
                        if attention and at[t] == X1T_SPLIT_AT[t]:
                            split_x1T(att, t)
                    if ffn and slot <= KF:
                        silu(this, slot)
                    if following and slot == XT_SPLIT_AT:
                        dve.wait_ge(v_done.sem, v_done.at(att, TILES))
                        split_xT(nxt)
                    for t, group in tail_steps(i, slot, ffn, tail, Y2_AFTER):
                        residual2(group, t)
                    for t, group in tail_steps(i, slot, ffn, tail, Z_AFTER):
                        residual3(group, t)
                    for t, group in tail_steps(i, slot, ffn, tail, LAYERNORM_AFTER):
                        layernorm(group, t)

            prepare_constants()
            split_xT((0, 0))
            for unit in range(KD):
                dve.wait_ge(w_hi_done.sem, unit + 1)
                nc.vector.tensor_tensor(
                    w_lo[:, unit, :], stage[:, unit, :], plain(w_hi[:, unit, :]), ALU.subtract
                ).then_inc(watt_lo_done.sem, 1)
            all_iterations(dve, iteration)

        @block.gpsimd
        def _(pool):
            pool.sem_inc(x1_scaled.sem, TILES)

            def add_gamma2(this):
                pool.wait_ge(x_in.sem, x_in.at(this, 16))
                pool.wait_ge(z_done.sem, z_done.at((this[0], this[1] - 1), TILES))
                nc.gpsimd.tensor_tensor(
                    x_gamma2[:, :, :], x[:, :, :],
                    row("gamma2").unsqueeze(1).to_broadcast([P, TILES, D]), ALU.add,
                ).then_inc(x_gamma2_done.sem, 1)

            def add_bo(att):
                pool.wait_ge(x_in.sem, x_in.at(att, 16))
                pool.wait_ge(x1T_evacuated.sem, x1T_evacuated.at((att[0], att[1] - 1), TILES))
                pool.wait_ge(x1_scaled.sem, x1_scaled.at((att[0], att[1] - 1), TILES))
                nc.gpsimd.tensor_tensor(
                    y1[:, :, :], x[:, :, :],
                    row("bo").unsqueeze(1).to_broadcast([P, TILES, D]), ALU.add,
                ).then_inc(x_bo_done.sem, 1)

            def x1_and_b2(this, t):
                pool.wait_ge(y1_normalized.sem, y1_normalized.at(this, t + 1))
                pool.wait_ge(y2_done.sem, y2_done.at((this[0], this[1] - 1), t + 1))
                nc.gpsimd.tensor_tensor(x1_b2[:, t, :], y1[:, t, :], row("alpha1"), ALU.mult).then_inc(x1_scaled.sem, 1)
                pool.wait_ge(x1_scaled.sem, x1_scaled.at(this, t + 1))
                pool.wait_ge(b2_gamma1_done.sem, 1)
                nc.gpsimd.tensor_tensor(x1_b2[:, t, :], x1_b2[:, t, :], row("b2"), ALU.add).then_inc(x1_b2_done.sem, 1)

            def inverse_rms(group, t, norm, squares_done, mean_done, rstd_done):
                pool.wait_ge(squares_done.sem, squares_done.at(group, t + 1))
                nc.gpsimd.tensor_tensor(
                    stats[:, norm, 1:2], stats[:, norm, 0:1], rms_eps[:, :], ALU.add
                ).then_inc(mean_done.sem, 1)
                pool.wait_ge(mean_done.sem, mean_done.at(group, t + 1))
                nc.gpsimd.tensor_tensor(stats[:, norm, 2:3], stats[:, norm, 1:2], minus_half[:, :], ALU.pow).then_inc(rstd_done.sem, 1)

            def inverse_deviation(this, t):
                pool.wait_ge(moments_done.sem, moments_done.at(this, t + 1))
                nc.gpsimd.tensor_tensor(ln_stats[:, 0:1], moments[:, 1:2], ln_eps[:, :], ALU.add).then_inc(var_done.sem, 1)
                pool.wait_ge(var_done.sem, var_done.at(this, t + 1))
                nc.gpsimd.tensor_tensor(ln_stats[:, 1:2], ln_stats[:, 0:1], minus_half[:, :], ALU.pow).then_inc(rstd3_done.sem, 1)

            def split_lo(unit):
                pool.wait_ge(w_hi_done.sem, unit + 1)
                nc.gpsimd.tensor_tensor(
                    w_lo[:, unit, :], stage[:, unit % STAGES, :], plain(w_hi[:, unit, :]), ALU.subtract
                ).then_inc(w12_lo_done.sem, 1)

            def iteration(i, following, attention, ffn, tail):
                before, this, att = (i, -1), (i, 0), (i, 1)
                if tail:
                    inverse_rms(before, 1, 1, squares2_done, mean2_done, rstd2_done)
                if ffn:
                    x1_and_b2(this, 0)
                if tail:
                    inverse_deviation(before, 1)
                if ffn:
                    x1_and_b2(this, 1)
                    add_gamma2(this)
                if attention:
                    add_bo(att)
                    if not ffn:
                        for unit in range(KD, 2 * KD):
                            split_lo(unit)
                    inverse_rms(att, 0, 0, squares1_done, mean1_done, rstd1_done)
                if ffn:
                    inverse_rms(this, 0, 1, squares2_done, mean2_done, rstd2_done)
                    inverse_deviation(this, 0)
                if attention:
                    if not ffn:
                        for unit in range(2 * KD, UNITS):
                            split_lo(unit)
                    inverse_rms(att, 1, 0, squares1_done, mean1_done, rstd1_done)

            pool.wait_ge(consts_ready.sem, 1)
            pool.wait_ge(rows_in.sem, 16)
            nc.gpsimd.tensor_tensor(row("b2"), row("b2"), row("gamma1"), ALU.add).then_inc(b2_gamma1_done.sem, 1)
            all_iterations(pool, iteration)


def kernel(**inputs):
    import numpy as np
    import concourse.bacc as bacc
    from concourse.bass_utils import run_bass_kernel_spmd

    given = {name.removeprefix("L0_gnn_"): np.asarray(a) for name, a in inputs.items()}
    x, adj = given["x"], given["adj"]
    B, N, D = x.shape
    G = B // TILES
    dh = D // HEADS
    kd = D // P
    spare = dh // kd

    order = []
    for c in range(kd):
        for odd in range(2):
            order += [(2 * c + odd) * dh + d for d in range(dh)]
            order += [(2 * kd + odd) * dh + c * spare + d for d in range(spare)]

    def by_chunk(a):
        return a.reshape(-1, P).T

    arrays = {
        "xT_in": x.reshape(G, TILES * N, kd, P).transpose(0, 3, 2, 1).reshape(G, P, kd * TILES * N),
        "x_in": x.reshape(G, TILES, N, D).transpose(0, 2, 1, 3).reshape(G, N, TILES * D),
        "adj_in": adj.reshape(G, TILES, N, N).transpose(0, 2, 1, 3).reshape(G, N, TILES * N),
        "watt_in": np.concatenate(
            [given[w][:, order[c * P : (c + 1) * P]] for c in range(kd) for w in ("wq", "wk")]
            + [given["wv"], given["wo"]], axis=1),
        "w1_in": given["w1"],
        "w2_in": given["w2"],
        "cols_in": np.concatenate(
            [by_chunk(given["bq"][order]), by_chunk(given["bk"][order]), by_chunk(given["b1"]),
             by_chunk(given["alpha1"]), by_chunk(given["gamma1"])], axis=1),
        "rows_in": np.broadcast_to(np.stack([given[n] for n in ROW_NAMES]), (P, len(ROW_NAMES), D)),
        "ident_in": np.eye(P, dtype=np.float32),
    }
    arrays = {name: np.ascontiguousarray(a) for name, a in arrays.items()}
    nc = bacc.Bacc("TRN2", target_bir_lowering=False, num_devices=1)
    args = [nc.dram_tensor(name, a.shape, mybir.dt.from_np(a.dtype), kind="ExternalInput").ap() for name, a in arrays.items()]
    out = nc.dram_tensor("out", (G, P, TILES * D), F32, kind="ExternalOutput").ap()
    build(nc, *args, out)
    result = run_bass_kernel_spmd(nc, [arrays], core_ids=[0]).results[0]["out"]
    return result.reshape(G, N, TILES, D).transpose(0, 2, 1, 3).reshape(B, N, D)
```

```python
from contextlib import ExitStack

import concourse.bass as bass
from concourse import mybir

P = 128
F32 = mybir.dt.float32
F32R = mybir.dt.float32r
ALU = mybir.AluOpType
ACT = mybir.ActivationFunctionType
AX_X = mybir.AxisListType.X

HEADS = 8
TILES = 2
RMS_EPS = 1e-6
LN_EPS = 1e-5

COL_NAMES = ("bq", "bk", "b1", "alpha1", "gamma1")
ROW_NAMES = ("bv", "bo", "alpha1", "gamma1", "b2", "alpha2", "gamma2")

BESIDE_FFN = {
    "qkv": (0, 0, 1, 1, 2, 2, 3, 3),
    "scores": (3, 10),
    "probsT": (8, 15),
    "context": (10, 17),
    "ctxT": (11, 18),
    "attention_out": (14, 20),
    "x1T": (16, 23),
    "exp": ((4, 4, 4, 5), (11, 11, 12, 12)),
    "probsT_half0": (7, 14),
    "ctxT_hi": (11, 17),
    "squares1": (13, 18),
    "y1_normalized": (14, 18),
    "x1T_evacuated": (17, 18),
    "bias": ((3, 3), (10, 11)),
    "probsT_half1": (6, 14),
    "context_normalized": (8, 16),
    "ctxT_lo": (11, 18),
    "y1": (12, 21),
    "x1T_split": (15, 21),
    "xT_split": 7,
}
ALONE = {
    "qkv": (0, 0, 0, 1, 1, 1, 2, 4),
    "next_qkv": (9, 9, 12, 13, 14, 15, 17, 18),
    "scores": (2, 8),
    "probsT": (6, 12),
    "context": (10, 15),
    "ctxT": (12, 17),
    "attention_out": (12, 19),
    "x1T": (16, 21),
    "w_split": (2, 4, 5, 9, 10, 11),
    "exp": ((2, 3, 3, 4), (9, 10, 11, 11)),
    "probsT_half0": (4, 12),
    "ctxT_hi": (10, 14),
    "squares1": (12, 16),
    "y1_normalized": (13, 18),
    "x1T_evacuated": (13, 18),
    "bias": ((0, 1), (6, 12)),
    "probsT_half1": (4, 14),
    "context_normalized": (8, 14),
    "ctxT_lo": (9, 16),
    "y1": (14, 23),
    "x1T_split": (22, 23),
    "xT_split": 5,
}
Y2_AFTER = 0
SQUARES2_AFTER = 0
Z_AFTER = 1
LAYERNORM_AFTER = 5


class Signal:

    def __init__(self, sem, n, primed=False):
        self.sem, self.n, self.primed = sem, n, primed

    def at(self, group, event):
        i, offset = group
        return i * self.n + (offset + self.primed) * self.n + event


def build(nc, xT_d, x_d, adj_d, watt_d, w1_d, w2_d, cols_d, rows_d, ident_d, out_d):
    G = x_d.shape[0]
    D = watt_d.shape[0]
    FF = w1_d.shape[1]
    KD = D // P
    KF = FF // P
    DH = D // HEADS
    NT = TILES * P
    SCALE = float(DH) ** -0.5
    UNIT = 4 * D
    assert UNIT == FF and KF % 4 == 0
    UNITS = 2 * KD + KF // 4
    QK = 2 * KD
    F2_PARTS = KF // 2
    SLOTS = KF + TILES * F2_PARTS
    HALF = HEADS // 2
    RING = UNIT // (2 * NT)
    PAIRS = KD

    col_at, at = {}, 0
    for name in COL_NAMES:
        col_at[name] = at
        at += KF if name == "b1" else KD

    with ExitStack() as ctx:

        def sb(name, shape, dt=F32):
            return ctx.enter_context(nc.sbuf_tensor(name, shape, dt))

        def ps(name, shape):
            return ctx.enter_context(nc.psum_tensor(name, shape, F32))

        def signal(name, n, primed=False):
            return Signal(ctx.enter_context(nc.semaphore(name)), n, primed)

        w_hi = sb("w_hi", [P, UNITS, UNIT], F32R)
        w_lo = sb("w_lo", [P, UNITS, UNIT], F32R)
        cols = sb("cols", [P, at])
        cols_scaled = sb("cols_scaled", [P, KD + KF])
        rows = sb("rows", [P, len(ROW_NAMES), D])
        ident = sb("ident", [P, P])
        minus_half = sb("minus_half", [P, 1])
        rms_eps = sb("rms_eps", [P, 1])
        ln_eps = sb("ln_eps", [P, 1])

        STAGES = 2 * KF * NT // UNIT + 2
        with nc.sbuf_tensor("stage", [P, STAGES, UNIT], F32) as stage:
            pass
        hT_hi = sb("hT_hi", [P, KF, NT], F32R)
        hT_lo = sb("hT_lo", [P, KF, NT], F32R)
        ffn_scratch = sb("ffn_scratch", [P, UNIT])
        tail_scratch = sb("tail_scratch", [P, UNIT])
        half_z = ffn_scratch[:, 0 : RING * NT].rearrange("p (r n) -> p r n", r=RING)
        hT = ffn_scratch[:, RING * NT : 2 * RING * NT].rearrange("p (r n) -> p r n", r=RING)
        x1_b2 = tail_scratch[:, 0 : TILES * D].rearrange("p (t n) -> p t n", t=TILES)
        y2 = tail_scratch[:, TILES * D : 2 * TILES * D].rearrange("p (t n) -> p t n", t=TILES)

        xT = sb("xT", [P, KD, NT])
        xT_hi = sb("xT_hi", [P, KD, NT], F32R)
        xT_lo = sb("xT_lo", [P, KD, NT], F32R)
        x = sb("x", [P, TILES, D])
        x_gamma2 = sb("x_gamma2", [P, TILES, D])
        adj = sb("adj", [P, TILES, P])
        qkT = sb("qkT", [P, QK, NT])
        qkT_last = sb("qkT_last", [P, 2, NT])
        v = sb("v", [P, TILES, HEADS, DH + 1])
        probs = sb("probs", [P, HEADS, P])
        probsT = sb("probsT", [P, HEADS, P])
        neg_max = sb("neg_max", [P, HEADS])
        inv_sum = sb("inv_sum", [P, HEADS])
        context = sb("context", [P, D])
        ctxT_hi = sb("ctxT_hi", [P, KD, P], F32R)
        ctxT_lo = sb("ctxT_lo", [P, KD, P], F32R)
        y1 = sb("y1", [P, TILES, D])
        x1T = sb("x1T", [P, KD, P])
        x1T_hi = sb("x1T_hi", [P, KD, NT], F32R)
        x1T_lo = sb("x1T_lo", [P, KD, NT], F32R)
        squares1_out = sb("squares1_out", [P, D], mybir.dt.bfloat16)
        squares2_out = sb("squares2_out", [P, D], mybir.dt.bfloat16)
        stats = sb("stats", [P, 2, 3])
        bn = sb("bn", [P, 6])
        moments = sb("moments", [P, 2])
        ln_stats = sb("ln_stats", [P, 2])

        BANKS = 4
        main = ps("main", [P, BANKS, 512])
        scores = ps("scores", [P, HEADS * P])
        small = ps("small", [P, 2, 512])

        watt_in = [signal(f"watt_in{n}", 0) for n in range(2 * KD)]
        w12_in = [signal(f"w12_in{n}", 0) for n in range(STAGES)]
        consts_in = signal("consts_in", 0)
        rows_in = signal("rows_in", 0)
        xT_in = signal("xT_in", 16)
        x_in = signal("x_in", 16)
        adj_in = signal("adj_in", 16)
        heads_moved = signal("heads_moved", 16 * 2 * PAIRS)
        out_stored = [signal(f"out_stored{t}", 16, primed=True) for t in range(TILES)]
        watt_hi_done = signal("watt_hi_done", 0)
        w12_hi_done = signal("w12_hi_done", 0)
        watt_lo_done = signal("watt_lo_done", 0)
        w12_lo_done = signal("w12_lo_done", 0)
        consts_ready = signal("consts_ready", 0)
        qk_done = signal("qk_done", QK)
        v_done = signal("v_done", TILES)
        scores_done = signal("scores_done", TILES)
        pt_done = signal("pt_done", TILES)
        ctx_done = signal("ctx_done", TILES)
        ctxT_done = signal("ctxT_done", TILES)
        wo_done = signal("wo_done", TILES)
        x1T_done = signal("x1T_done", TILES)
        f1_done = signal("f1_done", KF)
        f2_done = signal("f2_done", TILES)
        qk_evacuated = signal("qk_evacuated", QK)
        exp_done = signal("exp_done", TILES)
        pt_evacuated0 = signal("pt_evacuated0", TILES, primed=True)
        ctxT_hi_done = signal("ctxT_hi_done", TILES)
        squares1_done = signal("squares1_done", TILES)
        y1_normalized = signal("y1_normalized", TILES)
        x1T_evacuated = signal("x1T_evacuated", TILES, primed=True)
        half_z_done = signal("half_z_done", KF)
        tanh_done = signal("tanh_done", KF)
        squares2_done = signal("squares2_done", TILES)
        xT_hi_done = signal("xT_hi_done", 1)
        xT_split = signal("xT_split", 1)
        v_evacuated = signal("v_evacuated", TILES)
        scores_biased = signal("scores_biased", 2 * TILES)
        max_done = signal("max_done", 2 * TILES)
        pt_evacuated1 = signal("pt_evacuated1", TILES, primed=True)
        inv_sum_done = signal("inv_sum_done", TILES)
        context_done = signal("context_done", TILES)
        ctxT_lo_done = signal("ctxT_lo_done", TILES)
        y1_done = signal("y1_done", TILES, primed=True)
        x1T_hi_done = signal("x1T_hi_done", TILES)
        x1T_split = signal("x1T_split", TILES, primed=True)
        hT_done = signal("hT_done", KF)
        hT_hi_done = signal("hT_hi_done", KF)
        hT_split = signal("hT_split", KF, primed=True)
        y2_done = signal("y2_done", TILES, primed=True)
        x2_done = signal("x2_done", TILES)
        z_done = signal("z_done", TILES, primed=True)
        bn_done = signal("bn_done", TILES)
        moments_done = signal("moments_done", TILES)
        out_ready = signal("out_ready", TILES)
        b2_gamma1_done = signal("b2_gamma1_done", 0)
        x_gamma2_done = signal("x_gamma2_done", 1)
        x_bo_done = signal("x_bo_done", 1)
        x1_scaled = signal("x1_scaled", TILES, primed=True)
        x1_b2_done = signal("x1_b2_done", TILES)
        mean1_done = signal("mean1_done", TILES)
        rstd1_done = signal("rstd1_done", TILES)
        mean2_done = signal("mean2_done", TILES)
        rstd2_done = signal("rstd2_done", TILES)
        var_done = signal("var_done", TILES)
        rstd3_done = signal("rstd3_done", TILES)

        def projections(slot, attention, ffn, tail):
            at = BESIDE_FFN if ffn else ALONE
            steps = []
            for n in range(QK + TILES):
                if attention and (tail or not ffn) and at["qkv"][n] == slot:
                    steps.append((n, 1))
                if attention and not ffn and at["next_qkv"][n] == slot:
                    steps.append((n, 2))
            return steps

        def main_tiles(attention, ffn, tail):
            tiles = []
            for slot in range(SLOTS):
                for n, offset in projections(slot, attention, ffn, tail):
                    tiles.append(("qk", n, offset) if n < QK else ("v", n - QK, offset))
                if ffn and slot < KF:
                    tiles.append(("up", slot, 0))
                if ffn and slot == KF:
                    tiles += [None] * (-(len(tiles) + TILES) % BANKS)
                if ffn and slot >= KF and (slot - KF) % F2_PARTS == 0:
                    tiles.append(("down", (slot - KF) // F2_PARTS, 0))
            assert len(tiles) % BANKS == 0
            return tiles

        def tail_steps(i, slot, ffn, tail, after):
            steps = []
            for t in range(TILES):
                at = KF + (t + 1) * F2_PARTS - 1 + after
                if ffn and slot == at:
                    steps.append((t, (i, 0)))
                if tail and slot == at - SLOTS:
                    steps.append((t, (i, -1)))
            return steps

        def bank(tile, attention, ffn, tail):
            return main[:, main_tiles(attention, ffn, tail).index(tile) % BANKS, :]

        def row(name):
            return rows[:, ROW_NAMES.index(name), :]

        def col(name, c):
            return cols[:, col_at[name] + c : col_at[name] + c + 1]

        def plain(ap):
            return ap.bitcast(F32)

        def tokens(t):
            return slice(t * P, (t + 1) * P)

        def dram_group(ap, group):
            i, offset = group
            return ap[bass.ds(i + offset, 1), :, :].rearrange("g p n -> (g p) n")

        def weight_source(unit):
            if unit < KD:
                return watt_d[unit * P : (unit + 1) * P, :]
            if unit < 2 * KD:
                return w1_d[(unit - KD) * P : (unit - KD + 1) * P, :]
            first = (unit - 2 * KD) * 4 * P
            return w2_d[first : first + 4 * P, :].rearrange("(f p) n -> p f n", p=P)

        WATT_HALVES = [(unit, half) for half in (slice(0, 2 * D), slice(2 * D, 4 * D)) for unit in range(KD)]

        def w2_cols(f):
            return 2 * KD + f // 4, slice((f % 4) * D, (f % 4 + 1) * D)

        def all_iterations(engine, iteration):
            iteration(-1, True, True, False, False)
            iteration(0, True, True, True, False)
            with engine.Fori(1, G - 2) as i:
                iteration(i, True, True, True, True)
            iteration(G - 2, False, True, True, True)
            iteration(G - 1, False, False, True, True)
            iteration(G, False, False, False, True)

        block = ctx.enter_context(nc.Block())

        @block.sync
        def _(sp):
            for t in range(TILES):
                sp.sem_inc(out_stored[t].sem, 16)
            sp.dma_start(xT[:, :, :], dram_group(xT_d, (0, 0)).rearrange("p (k n) -> p k n", k=KD)).then_inc(xT_in.sem, 16)

            def load_w12(unit):
                dst = stage[:, unit % STAGES, :]
                if unit >= 2 * KD:
                    dst = dst.rearrange("p (f n) -> p f n", f=4)
                sp.dma_start(dst, weight_source(unit)).then_inc(w12_in[unit % STAGES].sem, 16)

            sp.dma_start(cols[:, :], cols_d).then_inc(consts_in.sem, 16)
            sp.dma_start(ident[:, :], ident_d).then_inc(consts_in.sem, 16)
            for n, (unit, half) in enumerate(WATT_HALVES):
                sp.dma_start(stage[:, unit, half], weight_source(unit)[:, half]).then_inc(watt_in[n].sem, 16)
            sp.dma_start(rows[:, :, :], rows_d).then_inc(rows_in.sem, 16)

            def store(group, t):
                sp.wait_ge(out_ready.sem, out_ready.at(group, t + 1))
                sp.dma_start(
                    dram_group(out_d, group)[:, t * D : (t + 1) * D], y2[:, t, :]
                ).then_inc(out_stored[t].sem, 16)

            def iteration(i, following, attention, ffn, tail):
                before, this, att, nxt = (i, -1), (i, 0), (i, 1), (i, 2)
                if attention:
                    if ffn:
                        sp.wait_ge(scores_biased.sem, scores_biased.at(this, 2 * TILES))
                    sp.dma_start(adj[:, :, :], dram_group(adj_d, att).rearrange("p (t n) -> p t n", t=TILES)).then_inc(adj_in.sem, 16)
                if following:
                    sp.wait_ge(xT_split.sem, xT_split.at(att, 1))
                    sp.dma_start(xT[:, :, :], dram_group(xT_d, nxt).rearrange("p (k n) -> p k n", k=KD)).then_inc(xT_in.sem, 16)
                if attention:
                    spare = DH // PAIRS
                    for c in range(PAIRS):
                        sp.wait_ge(qk_evacuated.sem, qk_evacuated.at(att, 2 * c + 2))
                        for half in (0, 64):
                            sp.dma_start(
                                qkT_last[half + c * spare : half + (c + 1) * spare, :, :],
                                qkT[half + DH : half + DH + spare, 2 * c : 2 * c + 2, :],
                            ).then_inc(heads_moved.sem, 16)
                if attention and not ffn:
                    for unit in range(KD, UNITS):
                        if unit == STAGES:
                            sp.wait_ge(watt_lo_done.sem, 2 * KD)
                        load_w12(unit)
                if tail:
                    store(before, 1)
                if attention:
                    if ffn:
                        sp.wait_ge(x_gamma2_done.sem, x_gamma2_done.at(this, 1))
                    sp.dma_start(x[:, :, :], dram_group(x_d, att).rearrange("p (t n) -> p t n", t=TILES)).then_inc(x_in.sem, 16)
                if ffn:
                    store(this, 0)

            all_iterations(sp, iteration)
            for t in range(TILES):
                sp.wait_ge(out_stored[t].sem, out_stored[t].at((G - 1, 0), 16))

        @block.tensor
        def _(pe):
            HI_LO = ((0, 0), (0, 1), (1, 0))

            def product(out, left, right, steps, first, last):
                for n, step in enumerate(steps):
                    for m, (a, b) in enumerate(HI_LO):
                        done = nc.tensor.matmul(
                            out,
                            left[a](step),
                            right[b](step),
                            start=first and n == 0 and m == 0,
                            stop=last and n == len(steps) - 1 and m == 2,
                        )
                return done

            def free_bank(i, tile, attention, ffn, tail):
                tiles = main_tiles(attention, ffn, tail)
                earlier = tiles[: tiles.index(tile)]
                step_back = 0
                bank_users = [tile for tile in earlier[-BANKS::-BANKS] if tile]
                if not bank_users:
                    step_back = 1
                    earlier = (main_tiles(True, tail, tail) if ffn else []) + earlier
                    bank_users = [tile for tile in earlier[-BANKS::-BANKS] if tile]
                if not bank_users:
                    return
                kind, n, offset = bank_users[0]
                if kind == "qk":
                    pe.wait_ge(qk_evacuated.sem, qk_evacuated.at((i, offset - step_back), n + 1))
                if kind == "v":
                    pe.wait_ge(v_evacuated.sem, v_evacuated.at((i, offset - step_back), n + 1))
                if kind == "up":
                    pe.wait_ge(half_z_done.sem, half_z_done.at((i, -step_back), n + 1))
                if kind == "down":
                    pe.wait_ge(y2_done.sem, y2_done.at((i, -step_back), n + 1))

            def add_qk(n, steps, out):
                return product(
                    out[:, 0:NT],
                    [lambda k, w=w: w[:, k, tokens(n)] for w in (w_hi, w_lo)],
                    [lambda k, a=a: a[:, k, :] for a in (xT_hi, xT_lo)],
                    steps, steps[0] == 0, steps[-1] == KD - 1,
                )

            def first_projections():
                pe.wait_ge(xT_split.sem, xT_split.at((0, 0), 1))
                for k in range(KD):
                    pe.wait_ge(watt_lo_done.sem, k + 1)
                    for n in range(BANKS):
                        done = add_qk(n, [k], bank(("qk", n, 1), True, False, False))
                        if k == KD - 1:
                            done.then_inc(qk_done.sem, 1)

            def project_qk(att, n, out):
                if n == 0:
                    pe.wait_ge(xT_split.sem, xT_split.at(att, 1))
                add_qk(n, range(KD), out).then_inc(qk_done.sem, 1)

            def project_v(att, t, out):
                product(
                    out[:, 0:D],
                    [lambda k, a=a: a[:, k, tokens(t)] for a in (xT_hi, xT_lo)],
                    [lambda k, w=w: w[:, k, 2 * D : 3 * D] for w in (w_hi, w_lo)],
                    range(KD), True, True,
                ).then_inc(v_done.sem, 1)

            def score_step(att, t):
                if t == 0:
                    pe.wait_ge(qk_evacuated.sem, qk_evacuated.at(att, QK))
                    pe.wait_ge(heads_moved.sem, heads_moved.at(att, heads_moved.n))
                if t == 0:
                    group, batches = (att[0], att[1] - 1), TILES
                else:
                    group, batches = att, t
                pe.wait_ge(pt_evacuated0.sem, pt_evacuated0.at(group, batches))
                pe.wait_ge(pt_evacuated1.sem, pt_evacuated1.at(group, batches))
                for h in range(HEADS):
                    c, odd = divmod(h, 2)
                    at = slice(64 * odd, 64 * odd + DH)
                    if c < PAIRS:
                        q, k = qkT[at, 2 * c, tokens(t)], qkT[at, 2 * c + 1, tokens(t)]
                    else:
                        q, k = qkT_last[at, 0, tokens(t)], qkT_last[at, 1, tokens(t)]
                    j = odd * HALF + c
                    done = nc.tensor.matmul(scores[:, tokens(j)], q, k, start=True, stop=True)
                done.then_inc(scores_done.sem, 1)

            def transpose_probs(att, t):
                pe.wait_ge(exp_done.sem, exp_done.at(att, t + 1))
                for j in range(HEADS):
                    done = nc.tensor.transpose(scores[:, tokens(j)], probs[:, j, :], ident[:, :])
                done.then_inc(pt_done.sem, 1)

            def context_step(att, t):
                pe.wait_ge(pt_evacuated0.sem, pt_evacuated0.at(att, t + 1))
                pe.wait_ge(pt_evacuated1.sem, pt_evacuated1.at(att, t + 1))
                if t == 0:
                    pe.wait_ge(v_evacuated.sem, v_evacuated.at(att, TILES))
                    pe.wait_ge(y1_done.sem, y1_done.at((att[0], att[1] - 1), TILES))
                else:
                    pe.wait_ge(y1_done.sem, y1_done.at(att, t))
                for h in range(HEADS):
                    j = (h % 2) * HALF + h // 2
                    done = nc.tensor.matmul(
                        small[:, 0, h * (DH + 1) : (h + 1) * (DH + 1)],
                        probsT[:, j, :], v[:, t, h, :], start=True, stop=True,
                    )
                done.then_inc(ctx_done.sem, 1)

            def transpose_context(att, t):
                pe.wait_ge(context_done.sem, context_done.at(att, t + 1))
                if t == 0:
                    pe.wait_ge(x1T_evacuated.sem, x1T_evacuated.at((att[0], att[1] - 1), TILES))
                else:
                    pe.wait_ge(x1T_evacuated.sem, x1T_evacuated.at(att, t))
                for c in range(KD):
                    done = nc.tensor.transpose(small[:, 1, tokens(c)], context[:, tokens(c)], ident[:, :])
                done.then_inc(ctxT_done.sem, 1)

            def output_projection(att, t):
                pe.wait_ge(ctxT_lo_done.sem, ctxT_lo_done.at(att, t + 1))
                product(
                    small[:, 0, 0:D],
                    [lambda k, a=a: a[:, k, :] for a in (ctxT_hi, ctxT_lo)],
                    [lambda k, w=w: w[:, k, 3 * D : 4 * D] for w in (w_hi, w_lo)],
                    range(KD), True, True,
                ).then_inc(wo_done.sem, 1)

            def transpose_x1(att, t):
                pe.wait_ge(y1_normalized.sem, y1_normalized.at(att, t + 1))
                for c in range(KD):
                    done = nc.tensor.transpose(small[:, 1, tokens(c)], y1[:, t, tokens(c)], ident[:, :])
                done.then_inc(x1T_done.sem, 1)

            def ffn_up(this, f, out):
                if f == 0:
                    pe.wait_ge(x1T_split.sem, x1T_split.at(this, TILES))
                product(
                    out[:, 0:NT],
                    [lambda k, w=w: w[:, KD + k, tokens(f)] for w in (w_hi, w_lo)],
                    [lambda k, a=a: a[:, k, :] for a in (x1T_hi, x1T_lo)],
                    range(KD), True, True,
                ).then_inc(f1_done.sem, 1)

            def ffn_down(this, t, part, out):
                if t == 0:
                    pe.wait_ge(hT_split.sem, hT_split.at(this, 2 * part + 2))
                last = part == F2_PARTS - 1
                done = product(
                    out[:, 0:D],
                    [lambda f, a=a: a[:, f, tokens(t)] for a in (hT_hi, hT_lo)],
                    [lambda f, w=w: w[:, w2_cols(f)[0], w2_cols(f)[1]] for w in (w_hi, w_lo)],
                    (2 * part, 2 * part + 1), part == 0, last,
                )
                if last:
                    done.then_inc(f2_done.sem, 1)

            def iteration(i, following, attention, ffn, tail):
                this, att = (i, 0), (i, 1)
                at = BESIDE_FFN if ffn else ALONE
                for slot in range(SLOTS if attention or ffn else 0):
                    for n, offset in projections(slot, attention, ffn, tail):
                        if not ffn and offset == 1 and n < BANKS:
                            continue
                        tile = ("qk", n, offset) if n < QK else ("v", n - QK, offset)
                        free_bank(i, tile, attention, ffn, tail)
                        if n < QK:
                            project_qk((i, offset), n, bank(tile, attention, ffn, tail))
                        else:
                            if not ffn:
                                pe.wait_ge(watt_lo_done.sem, 2 * KD)
                            project_v((i, offset), n - QK, bank(tile, attention, ffn, tail))
                    for t in range(TILES):
                        if attention and slot == at["scores"][t]:
                            score_step(att, t)
                        if attention and slot == at["probsT"][t]:
                            transpose_probs(att, t)
                        if attention and slot == at["context"][t]:
                            context_step(att, t)
                        if attention and slot == at["ctxT"][t]:
                            transpose_context(att, t)
                        if attention and slot == at["attention_out"][t]:
                            output_projection(att, t)
                        if attention and slot == at["x1T"][t]:
                            transpose_x1(att, t)
                    if ffn and not tail and slot == 0:
                        pe.wait_ge(w12_lo_done.sem, UNITS - KD)
                    if ffn and slot < KF:
                        free_bank(i, ("up", slot, 0), attention, ffn, tail)
                        ffn_up(this, slot, bank(("up", slot, 0), attention, ffn, tail))
                    if ffn and slot >= KF:
                        t, part = divmod(slot - KF, F2_PARTS)
                        if part == 0:
                            free_bank(i, ("down", t, 0), attention, ffn, tail)
                        ffn_down(this, t, part, bank(("down", t, 0), attention, ffn, tail))

            first_projections()
            pe.wait_ge(consts_ready.sem, 1)
            iteration(-1, True, True, False, False)
            iteration(0, True, True, True, False)
            with pe.Fori(1, G - 2) as i:
                iteration(i, True, True, True, True)
            iteration(G - 2, False, True, True, True)
            iteration(G - 1, False, False, True, True)

        @block.scalar
        def _(act):
            act.sem_inc(x1T_evacuated.sem, TILES)
            act.sem_inc(pt_evacuated0.sem, TILES)

            def split_hi(unit):
                act.wait_ge(w12_in[unit % STAGES].sem, 16)
                nc.scalar.copy(w_hi[:, unit, :], stage[:, unit % STAGES, :]).then_inc(w12_hi_done.sem, 1)

            def evacuate_qk(att, n, source):
                act.wait_ge(qk_done.sem, qk_done.at(att, n + 1))
                c = n // 2
                if n % 2 == 0:
                    bias, scale = cols_scaled[:, c : c + 1], SCALE
                else:
                    bias, scale = col("bk", c), 1.0
                nc.scalar.activation(qkT[:, n, :], source[:, 0:NT], ACT.Identity, bias=bias, scale=scale).then_inc(qk_evacuated.sem, 1)

            def exponentials(att, t, quarter):
                act.wait_ge(max_done.sem, max_done.at(att, 2 * t + quarter // 2 + 1))
                for j in range(quarter * HEADS // 4, (quarter + 1) * HEADS // 4):
                    done = nc.scalar.activation(probs[:, j, :], probs[:, j, :], ACT.Exp, bias=neg_max[:, j : j + 1])
                if quarter == 3:
                    done.then_inc(exp_done.sem, 1)

            def evacuate_probsT(att, t):
                act.wait_ge(pt_done.sem, pt_done.at(att, t + 1))
                nc.scalar.copy(probsT[:, 0:HALF, :], scores[:, 0 : HALF * P].rearrange("p (j n) -> p j n", j=HALF)).then_inc(pt_evacuated0.sem, 1)

            def context_hi(att, t):
                act.wait_ge(ctxT_done.sem, ctxT_done.at(att, t + 1))
                nc.scalar.copy(ctxT_hi[:, :, :], small[:, 1, 0:D].rearrange("p (c n) -> p c n", c=KD)).then_inc(ctxT_hi_done.sem, 1)

            def squares1(att, t):
                act.wait_ge(y1_done.sem, y1_done.at(att, t + 1))
                nc.scalar.activation(squares1_out[:, :], y1[:, t, :], ACT.Square, scale=D**-0.5, accum_out=stats[:, 0, 0:1]).then_inc(squares1_done.sem, 1)

            def normalize1(att, t):
                act.wait_ge(rstd1_done.sem, rstd1_done.at(att, t + 1))
                nc.scalar.activation(y1[:, t, :], y1[:, t, :], ACT.Copy, scale=stats[:, 0, 2:3]).then_inc(y1_normalized.sem, 1)

            def evacuate_x1T(att, t):
                act.wait_ge(x1T_done.sem, x1T_done.at(att, t + 1))
                if t == 0:
                    act.wait_ge(x1T_split.sem, x1T_split.at((att[0], att[1] - 1), TILES))
                else:
                    act.wait_ge(x1T_split.sem, x1T_split.at(att, t))
                for c in range(KD):
                    done = nc.scalar.activation(x1T[:, c, :], small[:, 1, tokens(c)], ACT.Identity, bias=col("gamma1", c), scale=col("alpha1", c))
                done.then_inc(x1T_evacuated.sem, 1)

            def silu_parts(this, f, source):
                act.wait_ge(f1_done.sem, f1_done.at(this, f + 1))
                if f >= RING:
                    act.wait_ge(hT_split.sem, hT_split.at(this, f - RING + 1))
                else:
                    act.wait_ge(hT_split.sem, hT_split.at((this[0], this[1] - 1), KF - RING + f + 1))
                nc.scalar.activation(half_z[:, f % RING, :], source[:, 0:NT], ACT.Identity, bias=cols_scaled[:, KD + f : KD + f + 1], scale=0.5).then_inc(half_z_done.sem, 1)
                act.wait_ge(half_z_done.sem, half_z_done.at(this, f + 1))
                nc.scalar.activation(hT[:, f % RING, :], half_z[:, f % RING, :], ACT.Tanh).then_inc(tanh_done.sem, 1)

            def squares2(this, t):
                act.wait_ge(y2_done.sem, y2_done.at(this, t + 1))
                nc.scalar.activation(squares2_out[:, :], y2[:, t, :], ACT.Square, scale=D**-0.5, accum_out=stats[:, 1, 0:1]).then_inc(squares2_done.sem, 1)

            def iteration(i, following, attention, ffn, tail):
                this, att = (i, 0), (i, 1)
                at = BESIDE_FFN if ffn else ALONE
                for slot in range(SLOTS):
                    if attention and not ffn and slot in at["w_split"]:
                        split_hi(KD + at["w_split"].index(slot))
                    for n, offset in projections(slot, attention, ffn, tail):
                        if n < QK:
                            evacuate_qk((i, offset), n, bank(("qk", n, offset), attention, ffn, tail))
                    for t in range(TILES):
                        for quarter in range(4):
                            if attention and slot == at["exp"][t][quarter]:
                                exponentials(att, t, quarter)
                        if attention and slot == at["probsT_half0"][t]:
                            evacuate_probsT(att, t)
                        if attention and slot == at["ctxT_hi"][t]:
                            context_hi(att, t)
                        if attention and slot == at["squares1"][t]:
                            squares1(att, t)
                        if attention and slot == at["y1_normalized"][t]:
                            normalize1(att, t)
                        if attention and slot == at["x1T_evacuated"][t]:
                            evacuate_x1T(att, t)
                    if ffn and slot < KF:
                        silu_parts(this, slot, bank(("up", slot, 0), attention, ffn, tail))
                    for t, group in tail_steps(i, slot, ffn, tail, SQUARES2_AFTER):
                        squares2(group, t)

            for n, (unit, half) in enumerate(WATT_HALVES):
                act.wait_ge(watt_in[n].sem, 16)
                nc.scalar.copy(w_hi[:, unit, half], stage[:, unit, half]).then_inc(watt_hi_done.sem, 1)
            act.wait_ge(consts_ready.sem, 1)
            all_iterations(act, iteration)

        @block.vector
        def _(dve):
            for s in (pt_evacuated1, y1_done, x1T_split, hT_split, y2_done, z_done):
                dve.sem_inc(s.sem, s.n)

            def split(source, hi, lo, hi_done, lo_done, group, event):
                nc.vector.tensor_copy(hi, source).then_inc(hi_done.sem, 1)
                dve.wait_ge(hi_done.sem, hi_done.at(group, event))
                nc.vector.tensor_tensor(lo, source, plain(hi), ALU.subtract).then_inc(lo_done.sem, 1)

            def split_xT(group):
                dve.wait_ge(xT_in.sem, xT_in.at(group, 16))
                split(xT[:, :, :], xT_hi[:, :, :], xT_lo[:, :, :], xT_hi_done, xT_split, group, 1)

            def prepare_constants():
                dve.wait_ge(consts_in.sem, 32)
                nc.vector.tensor_scalar(cols_scaled[:, 0:KD], cols[:, 0:KD], SCALE, None, ALU.mult)
                nc.vector.tensor_scalar(cols_scaled[:, KD:], cols[:, col_at["b1"] : col_at["b1"] + KF], 0.5, None, ALU.mult)
                nc.vector.memset(v[:, :, :, DH : DH + 1], 1.0)
                nc.vector.memset(minus_half[:, :], -0.5)
                nc.vector.memset(rms_eps[:, :], RMS_EPS)
                nc.vector.memset(ln_eps[:, :], LN_EPS).then_inc(consts_ready.sem, 1)

            def evacuate_v(att, t, source):
                dve.wait_ge(v_done.sem, v_done.at(att, t + 1))
                nc.vector.tensor_tensor(
                    v[:, t, :, 0:DH],
                    source[:, 0:D].rearrange("p (h d) -> p h d", h=HEADS),
                    row("bv").rearrange("p (h d) -> p h d", h=HEADS), ALU.add,
                ).then_inc(v_evacuated.sem, 1)

            def bias_and_max(att, t, half):
                heads = slice(half * HALF, (half + 1) * HALF)
                dve.wait_ge(scores_done.sem, scores_done.at(att, t + 1))
                if t == 0 and half == 0:
                    dve.wait_ge(adj_in.sem, adj_in.at(att, 16))
                nc.vector.tensor_tensor(
                    probs[:, heads, :],
                    scores[:, half * HALF * P : (half + 1) * HALF * P].rearrange("p (j n) -> p j n", j=HALF),
                    adj[:, t : t + 1, :].to_broadcast([P, HALF, P]), ALU.add,
                ).then_inc(scores_biased.sem, 1)
                dve.wait_ge(scores_biased.sem, scores_biased.at(att, 2 * t + half + 1))
                nc.vector.tensor_reduce(neg_max[:, heads], probs[:, heads, :], AX_X, ALU.max, negate=True).then_inc(max_done.sem, 1)

            def evacuate_probsT(att, t):
                dve.wait_ge(pt_done.sem, pt_done.at(att, t + 1))
                nc.vector.tensor_copy(
                    probsT[:, HALF:HEADS, :], scores[:, HALF * P : HEADS * P].rearrange("p (j n) -> p j n", j=HALF)
                ).then_inc(pt_evacuated1.sem, 1)

            def normalize_context(att, t):
                dve.wait_ge(ctx_done.sem, ctx_done.at(att, t + 1))
                sums = small[:, 0, 0 : HEADS * (DH + 1)].rearrange("p (h d) -> p h d", h=HEADS)
                nc.vector.reciprocal(inv_sum[:, :], sums[:, :, DH : DH + 1].rearrange("p h o -> p (h o)")).then_inc(inv_sum_done.sem, 1)
                dve.wait_ge(inv_sum_done.sem, inv_sum_done.at(att, t + 1))
                nc.vector.tensor_tensor(
                    context[:, :].rearrange("p (h d) -> p h d", h=HEADS),
                    sums[:, :, 0:DH],
                    inv_sum[:, :].unsqueeze(2).to_broadcast([P, HEADS, DH]), ALU.mult,
                ).then_inc(context_done.sem, 1)

            def context_lo(att, t):
                dve.wait_ge(ctxT_hi_done.sem, ctxT_hi_done.at(att, t + 1))
                nc.vector.tensor_tensor(
                    ctxT_lo[:, :, :], small[:, 1, 0:D].rearrange("p (c n) -> p c n", c=KD),
                    plain(ctxT_hi[:, :, :]), ALU.subtract,
                ).then_inc(ctxT_lo_done.sem, 1)

            def residual1(att, t):
                dve.wait_ge(wo_done.sem, wo_done.at(att, t + 1))
                if t == 0:
                    dve.wait_ge(x_bo_done.sem, x_bo_done.at(att, 1))
                nc.vector.tensor_tensor(y1[:, t, :], small[:, 0, 0:D], y1[:, t, :], ALU.add).then_inc(y1_done.sem, 1)

            def split_x1T(att, t):
                dve.wait_ge(x1T_evacuated.sem, x1T_evacuated.at(att, t + 1))
                split(x1T[:, :, :], x1T_hi[:, :, tokens(t)], x1T_lo[:, :, tokens(t)], x1T_hi_done, x1T_split, att, t + 1)

            def silu(this, f):
                if f < KF:
                    dve.wait_ge(tanh_done.sem, tanh_done.at(this, f + 1))
                    nc.vector.scalar_tensor_tensor(
                        hT[:, f % RING, :], hT[:, f % RING, :], 1.0, half_z[:, f % RING, :], ALU.add, ALU.mult
                    ).then_inc(hT_done.sem, 1)
                if f > 0:
                    dve.wait_ge(hT_hi_done.sem, hT_hi_done.at(this, f))
                    nc.vector.tensor_tensor(
                        hT_lo[:, f - 1, :], hT[:, (f - 1) % RING, :], plain(hT_hi[:, f - 1, :]), ALU.subtract
                    ).then_inc(hT_split.sem, 1)
                if f < KF:
                    dve.wait_ge(hT_done.sem, hT_done.at(this, f + 1))
                    nc.vector.tensor_copy(hT_hi[:, f, :], hT[:, f % RING, :]).then_inc(hT_hi_done.sem, 1)

            def residual2(this, t):
                dve.wait_ge(f2_done.sem, f2_done.at(this, t + 1))
                dve.wait_ge(x1_b2_done.sem, x1_b2_done.at(this, t + 1))
                dve.wait_ge(out_stored[t].sem, out_stored[t].at((this[0], this[1] - 1), 16))
                nc.vector.tensor_tensor(y2[:, t, :], main[:, BANKS - TILES + t, 0:D], x1_b2[:, t, :], ALU.add).then_inc(y2_done.sem, 1)

            def residual3(this, t):
                dve.wait_ge(rstd2_done.sem, rstd2_done.at(this, t + 1))
                nc.vector.scalar_tensor_tensor(
                    y2[:, t, :], y2[:, t, :], stats[:, 1, 2:3], row("alpha2"), ALU.mult, ALU.mult
                ).then_inc(x2_done.sem, 1)
                dve.wait_ge(x2_done.sem, x2_done.at(this, t + 1))
                if t == 0:
                    dve.wait_ge(x_gamma2_done.sem, x_gamma2_done.at(this, 1))
                nc.vector.tensor_tensor(y2[:, t, :], y2[:, t, :], x_gamma2[:, t, :], ALU.add).then_inc(z_done.sem, 1)
                dve.wait_ge(z_done.sem, z_done.at(this, t + 1))
                nc.vector.bn_stats(bn[:, :], y2[:, t, :]).then_inc(bn_done.sem, 1)
                dve.wait_ge(consts_ready.sem, 1)
                dve.wait_ge(bn_done.sem, bn_done.at(this, t + 1))
                nc.vector.bn_aggr(moments[:, :], bn[:, :]).then_inc(moments_done.sem, 1)

            def layernorm(this, t):
                dve.wait_ge(rstd3_done.sem, rstd3_done.at(this, t + 1))
                nc.vector.tensor_scalar(
                    y2[:, t, :], y2[:, t, :], moments[:, 0:1], ln_stats[:, 1:2], ALU.subtract, ALU.mult
                ).then_inc(out_ready.sem, 1)

            def iteration(i, following, attention, ffn, tail):
                before, this, att, nxt = (i, -1), (i, 0), (i, 1), (i, 2)
                at = BESIDE_FFN if ffn else ALONE
                for slot in range(SLOTS):
                    for n, offset in projections(slot, attention, ffn, tail):
                        if not ffn and (n, offset) == (QK, 1):
                            dve.wait_ge(rows_in.sem, 16)
                        if n >= QK:
                            evacuate_v((i, offset), n - QK, bank(("v", n - QK, offset), attention, ffn, tail))
                    for t in range(TILES):
                        for half in range(2):
                            if attention and slot == at["bias"][t][half]:
                                bias_and_max(att, t, half)
                        if attention and slot == at["probsT_half1"][t]:
                            evacuate_probsT(att, t)
                        if attention and slot == at["context_normalized"][t]:
                            normalize_context(att, t)
                        if attention and slot == at["ctxT_lo"][t]:
                            context_lo(att, t)
                        if attention and slot == at["y1"][t]:
                            residual1(att, t)
                        if attention and slot == at["x1T_split"][t]:
                            split_x1T(att, t)
                    if ffn and slot <= KF:
                        silu(this, slot)
                    if following and slot == at["xT_split"]:
                        dve.wait_ge(v_done.sem, v_done.at(att, TILES))
                        split_xT(nxt)
                    for t, group in tail_steps(i, slot, ffn, tail, Y2_AFTER):
                        residual2(group, t)
                    for t, group in tail_steps(i, slot, ffn, tail, Z_AFTER):
                        residual3(group, t)
                    for t, group in tail_steps(i, slot, ffn, tail, LAYERNORM_AFTER):
                        layernorm(group, t)

            prepare_constants()
            split_xT((0, 0))
            for n, (unit, half) in enumerate(WATT_HALVES):
                dve.wait_ge(watt_hi_done.sem, n + 1)
                nc.vector.tensor_tensor(
                    w_lo[:, unit, half], stage[:, unit, half], plain(w_hi[:, unit, half]), ALU.subtract
                ).then_inc(watt_lo_done.sem, 1)
            all_iterations(dve, iteration)

        @block.gpsimd
        def _(pool):
            pool.sem_inc(x1_scaled.sem, TILES)

            def add_gamma2(this):
                pool.wait_ge(x_in.sem, x_in.at(this, 16))
                pool.wait_ge(z_done.sem, z_done.at((this[0], this[1] - 1), TILES))
                nc.gpsimd.tensor_tensor(
                    x_gamma2[:, :, :], x[:, :, :],
                    row("gamma2").unsqueeze(1).to_broadcast([P, TILES, D]), ALU.add,
                ).then_inc(x_gamma2_done.sem, 1)

            def add_bo(att):
                pool.wait_ge(x_in.sem, x_in.at(att, 16))
                pool.wait_ge(x1T_evacuated.sem, x1T_evacuated.at((att[0], att[1] - 1), TILES))
                pool.wait_ge(x1_scaled.sem, x1_scaled.at((att[0], att[1] - 1), TILES))
                nc.gpsimd.tensor_tensor(
                    y1[:, :, :], x[:, :, :],
                    row("bo").unsqueeze(1).to_broadcast([P, TILES, D]), ALU.add,
                ).then_inc(x_bo_done.sem, 1)

            def x1_and_b2(this, t):
                pool.wait_ge(y1_normalized.sem, y1_normalized.at(this, t + 1))
                pool.wait_ge(y2_done.sem, y2_done.at((this[0], this[1] - 1), t + 1))
                nc.gpsimd.tensor_tensor(x1_b2[:, t, :], y1[:, t, :], row("alpha1"), ALU.mult).then_inc(x1_scaled.sem, 1)
                pool.wait_ge(x1_scaled.sem, x1_scaled.at(this, t + 1))
                pool.wait_ge(b2_gamma1_done.sem, 1)
                nc.gpsimd.tensor_tensor(x1_b2[:, t, :], x1_b2[:, t, :], row("b2"), ALU.add).then_inc(x1_b2_done.sem, 1)

            def inverse_rms(group, t, norm, squares_done, mean_done, rstd_done):
                pool.wait_ge(squares_done.sem, squares_done.at(group, t + 1))
                nc.gpsimd.tensor_tensor(
                    stats[:, norm, 1:2], stats[:, norm, 0:1], rms_eps[:, :], ALU.add
                ).then_inc(mean_done.sem, 1)
                pool.wait_ge(mean_done.sem, mean_done.at(group, t + 1))
                nc.gpsimd.tensor_tensor(stats[:, norm, 2:3], stats[:, norm, 1:2], minus_half[:, :], ALU.pow).then_inc(rstd_done.sem, 1)

            def inverse_deviation(this, t):
                pool.wait_ge(moments_done.sem, moments_done.at(this, t + 1))
                nc.gpsimd.tensor_tensor(ln_stats[:, 0:1], moments[:, 1:2], ln_eps[:, :], ALU.add).then_inc(var_done.sem, 1)
                pool.wait_ge(var_done.sem, var_done.at(this, t + 1))
                nc.gpsimd.tensor_tensor(ln_stats[:, 1:2], ln_stats[:, 0:1], minus_half[:, :], ALU.pow).then_inc(rstd3_done.sem, 1)

            def split_lo(unit):
                pool.wait_ge(w12_hi_done.sem, unit - KD + 1)
                nc.gpsimd.tensor_tensor(
                    w_lo[:, unit, :], stage[:, unit % STAGES, :], plain(w_hi[:, unit, :]), ALU.subtract
                ).then_inc(w12_lo_done.sem, 1)

            def iteration(i, following, attention, ffn, tail):
                before, this, att = (i, -1), (i, 0), (i, 1)
                if tail:
                    inverse_rms(before, 1, 1, squares2_done, mean2_done, rstd2_done)
                if ffn:
                    x1_and_b2(this, 0)
                if tail:
                    inverse_deviation(before, 1)
                if ffn:
                    x1_and_b2(this, 1)
                    add_gamma2(this)
                if attention and not ffn:
                    for unit in range(KD, 2 * KD):
                        split_lo(unit)
                if attention:
                    add_bo(att)
                    if not ffn:
                        for unit in range(2 * KD, UNITS):
                            split_lo(unit)
                    inverse_rms(att, 0, 0, squares1_done, mean1_done, rstd1_done)
                if ffn:
                    inverse_rms(this, 0, 1, squares2_done, mean2_done, rstd2_done)
                    inverse_deviation(this, 0)
                if attention:
                    inverse_rms(att, 1, 0, squares1_done, mean1_done, rstd1_done)

            pool.wait_ge(consts_ready.sem, 1)
            pool.wait_ge(rows_in.sem, 16)
            nc.gpsimd.tensor_tensor(row("b2"), row("b2"), row("gamma1"), ALU.add).then_inc(b2_gamma1_done.sem, 1)
            all_iterations(pool, iteration)


def kernel(**inputs):
    import numpy as np
    import concourse.bacc as bacc
    from concourse.bass_utils import run_bass_kernel_spmd

    given = {name.removeprefix("L0_gnn_"): np.asarray(a) for name, a in inputs.items()}
    x, adj = given["x"], given["adj"]
    B, N, D = x.shape
    G = B // TILES
    dh = D // HEADS
    kd = D // P
    spare = dh // kd

    order = []
    for c in range(kd):
        for odd in range(2):
            order += [(2 * c + odd) * dh + d for d in range(dh)]
            order += [(2 * kd + odd) * dh + c * spare + d for d in range(spare)]

    def by_chunk(a):
        return a.reshape(-1, P).T

    arrays = {
        "xT_in": x.reshape(G, TILES * N, kd, P).transpose(0, 3, 2, 1).reshape(G, P, kd * TILES * N),
        "x_in": x.reshape(G, TILES, N, D).transpose(0, 2, 1, 3).reshape(G, N, TILES * D),
        "adj_in": adj.reshape(G, TILES, N, N).transpose(0, 2, 1, 3).reshape(G, N, TILES * N),
        "watt_in": np.concatenate(
            [given[w][:, order[c * P : (c + 1) * P]] for c in range(kd) for w in ("wq", "wk")]
            + [given["wv"], given["wo"]], axis=1),
        "w1_in": given["w1"],
        "w2_in": given["w2"],
        "cols_in": np.concatenate(
            [by_chunk(given["bq"][order]), by_chunk(given["bk"][order]), by_chunk(given["b1"]),
             by_chunk(given["alpha1"]), by_chunk(given["gamma1"])], axis=1),
        "rows_in": np.broadcast_to(np.stack([given[n] for n in ROW_NAMES]), (P, len(ROW_NAMES), D)),
        "ident_in": np.eye(P, dtype=np.float32),
    }
    arrays = {name: np.ascontiguousarray(a) for name, a in arrays.items()}
    nc = bacc.Bacc("TRN2", target_bir_lowering=False, num_devices=1)
    args = [nc.dram_tensor(name, a.shape, mybir.dt.from_np(a.dtype), kind="ExternalInput").ap() for name, a in arrays.items()]
    out = nc.dram_tensor("out", (G, P, TILES * D), F32, kind="ExternalOutput").ap()
    build(nc, *args, out)
    result = run_bass_kernel_spmd(nc, [arrays], core_ids=[0]).results[0]["out"]
    return result.reshape(G, N, TILES, D).transpose(0, 2, 1, 3).reshape(B, N, D)
```
